# Optimizing a Trainium2 kernel written in Bass

```python
import numpy as np
import jax
import jax.numpy as jnp

def _softmax(x, axis=-1):
    return jax.nn.softmax(x, axis=axis)

def _gelu(x):
    return jax.nn.gelu(x, approximate=True)

def _silu(x):
    return jax.nn.silu(x)

def _sigmoid(x):
    return jax.nn.sigmoid(x)

def _layernorm(x, axis=-1, eps=1e-05):
    m = jnp.mean(x, axis=axis, keepdims=True)
    v = jnp.var(x, axis=axis, keepdims=True)
    return (x - m) / jnp.sqrt(v + eps)

def _scatter_add(tgt, idx, src, axis=0):
    return tgt.at[idx].add(src)

def _segment_sum(src, seg, n):
    return jax.ops.segment_sum(src, seg, n)
kernel_name = 'mk_gnn_resnorm_d4_gnn_r32_f0b73e'

def setup_inputs(seed: int=0):
    np.random.seed(seed)
    _w = jnp.asarray

    def _rec_inputs():
        import jax
        import jax.numpy as jnp
        _gk = jax.random.key(seed)
        x = -0.0003713 + 1 * jax.random.normal(jax.random.fold_in(_gk, 1), (3125, 128), jnp.float32)
        src = jax.random.randint(jax.random.fold_in(_gk, 2), (100000,), 0, 3125, jnp.int32)
        dst = jax.random.randint(jax.random.fold_in(_gk, 3), (100000,), 0, 3125, jnp.int32)
        _o = jnp.argsort(dst, stable=True)
        src = src[_o]
        dst = dst[_o]
        edge_attr_32 = 0.000196303 + 1.00016 * jax.random.normal(jax.random.fold_in(_gk, 12), (100000, 32), jnp.float32)
        edge_type_9 = jax.random.randint(jax.random.fold_in(_gk, 14), (100000,), 0, 9, jnp.int32)
        edge_weight = jax.random.uniform(jax.random.fold_in(_gk, 15), (100000,), jnp.float32, 0.0, 1)
        return (x, src, dst, edge_attr_32, edge_type_9, edge_weight)
    x, src, dst, edge_attr_32, edge_type_9, edge_weight = _rec_inputs()

    def _L0_gnn_setup():
        import jax, jax.numpy as jnp
        import numpy as np
        N_NODES = 3125
        DIM = 128
        N_EDGES = 20000
        key = jax.random.key(seed)
        k_x, k_e, k_w1, k_b1, k_w2, k_b2 = jax.random.split(key, 6)
        x = jax.random.normal(k_x, (N_NODES, DIM), dtype=jnp.float32)
        edge_index = jax.random.randint(k_e, (2, N_EDGES), 0, N_NODES, dtype=jnp.int64)
        s = 1.0 / np.sqrt(DIM)
        W1 = jax.random.uniform(k_w1, (DIM, DIM), minval=-s, maxval=s, dtype=jnp.float32)
        b1 = jax.random.uniform(k_b1, (DIM,), minval=-s, maxval=s, dtype=jnp.float32)
        W2 = jax.random.uniform(k_w2, (DIM, DIM), minval=-s, maxval=s, dtype=jnp.float32)
        b2 = jax.random.uniform(k_b2, (DIM,), minval=-s, maxval=s, dtype=jnp.float32)
        return {'x': x, 'edge_index': edge_index, 'W1': W1, 'b1': b1, 'W2': W2, 'b2': b2}
    _L0_gnn_all = _L0_gnn_setup()
    _L0_gnn_in = {k: v for k, v in _L0_gnn_all.items() if k in ('W1', 'b1', 'W2', 'b2')}
    del _L0_gnn_all

    def _L1_gnn_setup():
        import jax, jax.numpy as jnp
        import numpy as np
        N, E = (50000, 25000)
        D_IN, HID, H, C, E_DIM = (128, 128, 4, 32, 32)
        key = jax.random.key(seed)
        ks = jax.random.split(key, 16)

        def lin(k, fan_in, fan_out):
            return jax.random.normal(k, (fan_in, fan_out), jnp.float32) / np.sqrt(fan_in)
        return {'x': jax.random.normal(ks[0], (N, D_IN), jnp.float32), 'edge_index': jax.random.randint(ks[1], (2, E), 0, N, jnp.int32), 'edge_attr': jax.random.normal(ks[2], (E, E_DIM), jnp.float32), 'Wq': lin(ks[3], D_IN, HID), 'bq': jnp.zeros((HID,), jnp.float32), 'Wk': lin(ks[4], D_IN, HID), 'bk': jnp.zeros((HID,), jnp.float32), 'Wv': lin(ks[5], D_IN, HID), 'bv': jnp.zeros((HID,), jnp.float32), 'We': lin(ks[6], E_DIM, HID), 'Wskip': lin(ks[7], D_IN, HID), 'bskip': jnp.zeros((HID,), jnp.float32), 'W1': lin(ks[8], HID, HID), 'b1': jnp.zeros((HID,), jnp.float32), 'W2': lin(ks[9], HID, HID), 'b2': jnp.zeros((HID,), jnp.float32)}
    _L1_gnn_all = _L1_gnn_setup()
    _L1_gnn_in = {k: v for k, v in _L1_gnn_all.items() if k in ('Wq', 'bq', 'Wk', 'bk', 'Wv', 'bv', 'We', 'Wskip', 'bskip', 'W1', 'b1', 'W2', 'b2')}
    del _L1_gnn_all

    def _L2_gnn_setup():
        import jax, jax.numpy as jnp
        import numpy as np
        N_NODES = 3125
        D = 128
        N_EDGES = 50000
        N_LAYERS = 3

        def _spmm(vals, rows, cols, x, n):
            gathered = vals[:, None] * x[cols]
            return jax.ops.segment_sum(gathered, rows, num_segments=n)
        key = jax.random.key(seed)
        k1, k2, k3, k4 = jax.random.split(key, 4)
        emb = jax.random.normal(k1, (N_NODES, D), dtype=jnp.float32)
        vals = jax.random.uniform(k2, (N_EDGES,), dtype=jnp.float32)
        rows = jax.random.randint(k3, (N_EDGES,), 0, N_NODES, dtype=jnp.int64 if jax.config.jax_enable_x64 else jnp.int32)
        cols = jax.random.randint(k4, (N_EDGES,), 0, N_NODES, dtype=jnp.int64 if jax.config.jax_enable_x64 else jnp.int32)
        return {'emb': emb, 'vals': vals, 'rows': rows, 'cols': cols}
    _L2_gnn_all = _L2_gnn_setup()
    _L2_gnn_in = {k: v for k, v in _L2_gnn_all.items() if k in ()}
    del _L2_gnn_all

    def _L3_gnn_setup():
        import jax, jax.numpy as jnp
        import numpy as np
        N = 3125
        E = 128
        R = 9
        L = 3
        NE = 20000
        key = jax.random.key(seed)
        k = jax.random.split(key, 5)
        edge_index = jax.random.randint(k[0], (2, NE), 0, N, dtype=jnp.int64)
        edge_type = jax.random.randint(k[1], (NE,), 0, R, dtype=jnp.int64)
        embeddings = jax.random.normal(k[2], (N, E), dtype=jnp.float32)
        weights = jax.random.normal(k[3], (L, 2 * R, E, E), dtype=jnp.float32)
        biases = jax.random.normal(k[4], (L, 2 * R, E), dtype=jnp.float32)
        return {'edge_index': edge_index, 'edge_type': edge_type, 'embeddings': embeddings, 'weights': weights, 'biases': biases}
    _L3_gnn_all = _L3_gnn_setup()
    _L3_gnn_in = {k: v for k, v in _L3_gnn_all.items() if k in ('weights', 'biases')}
    del _L3_gnn_all
    return {'x': x, 'src': src, 'dst': dst, 'edge_attr_32': edge_attr_32, 'edge_type_9': edge_type_9, 'edge_weight': edge_weight, 'L0_gnn_W1': _L0_gnn_in['W1'], 'L0_gnn_b1': _L0_gnn_in['b1'], 'L0_gnn_W2': _L0_gnn_in['W2'], 'L0_gnn_b2': _L0_gnn_in['b2'], 'L1_gnn_Wq': _L1_gnn_in['Wq'], 'L1_gnn_bq': _L1_gnn_in['bq'], 'L1_gnn_Wk': _L1_gnn_in['Wk'], 'L1_gnn_bk': _L1_gnn_in['bk'], 'L1_gnn_Wv': _L1_gnn_in['Wv'], 'L1_gnn_bv': _L1_gnn_in['bv'], 'L1_gnn_We': _L1_gnn_in['We'], 'L1_gnn_Wskip': _L1_gnn_in['Wskip'], 'L1_gnn_bskip': _L1_gnn_in['bskip'], 'L1_gnn_W1': _L1_gnn_in['W1'], 'L1_gnn_b1': _L1_gnn_in['b1'], 'L1_gnn_W2': _L1_gnn_in['W2'], 'L1_gnn_b2': _L1_gnn_in['b2'], 'L3_gnn_weights': _L3_gnn_in['weights'], 'L3_gnn_biases': _L3_gnn_in['biases']}

def reference(x, src, dst, edge_attr_32, edge_type_9, edge_weight, L0_gnn_W1, L0_gnn_b1, L0_gnn_W2, L0_gnn_b2, L1_gnn_Wq, L1_gnn_bq, L1_gnn_Wk, L1_gnn_bk, L1_gnn_Wv, L1_gnn_bv, L1_gnn_We, L1_gnn_Wskip, L1_gnn_bskip, L1_gnn_W1, L1_gnn_b1, L1_gnn_W2, L1_gnn_b2, L3_gnn_weights, L3_gnn_biases):
    import jax
    import jax.numpy as jnp

    def _L0_gnn_ref(x, edge_index, W1, b1, W2, b2):
        import jax, jax.numpy as jnp
        import numpy as np
        N_NODES = 3125
        DIM = 128
        N_EDGES = 20000
        row, col = (edge_index[0], edge_index[1])
        n = x.shape[0]
        msg = x[col]
        summed = jax.ops.segment_sum(msg, row, num_segments=n)
        deg = jax.ops.segment_sum(jnp.ones((row.shape[0],), x.dtype), row, num_segments=n)
        agg = summed / jnp.maximum(deg, 1.0)[:, None]
        h = jax.nn.relu(agg @ W1.T + b1)
        return h @ W2.T + b2

    def _L1_gnn_ref(x, edge_index, edge_attr, Wq, bq, Wk, bk, Wv, bv, We, Wskip, bskip, W1, b1, W2, b2):
        import jax, jax.numpy as jnp
        import numpy as np
        N, E = (50000, 25000)
        D_IN, HID, H, C, E_DIM = (128, 128, 4, 32, 32)
        src, dst = (edge_index[0], edge_index[1])
        n = x.shape[0]
        q = (x @ Wq + bq).reshape(n, H, C)
        k = (x @ Wk + bk).reshape(n, H, C)
        v = (x @ Wv + bv).reshape(n, H, C)
        e = (edge_attr @ We).reshape(-1, H, C)
        kj = k[src] + e
        vj = v[src] + e
        alpha = jnp.einsum('ehc,ehc->eh', q[dst], kj) / np.sqrt(C)
        amax = jax.ops.segment_max(alpha, dst, num_segments=n)
        amax = jnp.where(jnp.isfinite(amax), amax, 0.0)
        ex = jnp.exp(alpha - amax[dst])
        denom = jax.ops.segment_sum(ex, dst, num_segments=n)
        alpha = ex / (denom[dst] + 1e-16)
        agg = jax.ops.segment_sum(vj * alpha[:, :, None], dst, num_segments=n)
        out = agg.reshape(n, HID) + (x @ Wskip + bskip)
        h = jax.nn.gelu(out @ W1 + b1, approximate=True)
        h = jax.nn.gelu(h @ W2 + b2, approximate=True)
        return out + h

    def _L2_gnn_ref(emb, vals, rows, cols):
        import jax, jax.numpy as jnp
        import numpy as np
        N_NODES = 3125
        D = 128
        N_EDGES = 50000
        N_LAYERS = 3

        def _spmm(vals, rows, cols, x, n):
            gathered = vals[:, None] * x[cols]
            return jax.ops.segment_sum(gathered, rows, num_segments=n)
        n = emb.shape[0]
        side = _spmm(vals, rows, cols, emb, n)
        light_out = (emb + N_LAYERS * side) / (N_LAYERS + 1)
        return light_out

    def _L3_gnn_ref(edge_index, edge_type, embeddings, weights, biases):
        import jax, jax.numpy as jnp
        import numpy as np
        N = 3125
        E = 128
        R = 9
        L = 3
        NE = 20000
        src, dst = (edge_index[0], edge_index[1])
        n_nodes = embeddings.shape[0]
        n_layers, r2 = (weights.shape[0], weights.shape[1])
        n_rel = r2 // 2
        hidden = embeddings
        for l in range(n_layers):
            hidden = embeddings
            ht = jnp.einsum('ne,reh->rnh', hidden, weights[l])
            msg_f = ht[edge_type, src] + biases[l][edge_type]
            out = jax.ops.segment_sum(msg_f, dst, num_segments=n_nodes)
            msg_b = ht[edge_type + n_rel, dst] + biases[l][edge_type + n_rel]
            out = out + jax.ops.segment_sum(msg_b, src, num_segments=n_nodes)
            hidden = out
        return hidden
    edge_index = jnp.stack([src, dst])
    x = _layernorm(x + _L0_gnn_ref(x, edge_index, L0_gnn_W1, L0_gnn_b1, L0_gnn_W2, L0_gnn_b2), axis=-1)
    x = _layernorm(x + _L1_gnn_ref(x, edge_index, edge_attr_32, L1_gnn_Wq, L1_gnn_bq, L1_gnn_Wk, L1_gnn_bk, L1_gnn_Wv, L1_gnn_bv, L1_gnn_We, L1_gnn_Wskip, L1_gnn_bskip, L1_gnn_W1, L1_gnn_b1, L1_gnn_W2, L1_gnn_b2), axis=-1)
    x = _layernorm(x + _L2_gnn_ref(x, edge_weight, src, dst), axis=-1)
    x = _layernorm(x + _L3_gnn_ref(edge_index, edge_type_9, x, L3_gnn_weights, L3_gnn_biases), axis=-1)
    return x

_drawn_inputs = setup_inputs


def setup_inputs(seed=0):
    import zlib

    import numpy as np

    out = dict(_drawn_inputs(seed))
    spreads = {'L1_gnn_bq': (0.0, 0.1),
     'L1_gnn_bk': (0.0, 0.1),
     'L1_gnn_bv': (0.0, 0.1),
     'L1_gnn_bskip': (0.0, 0.1),
     'L1_gnn_b1': (0.0, 0.1),
     'L1_gnn_b2': (0.0, 0.1)}
    factors = {}
    for name, (base, spread) in spreads.items():
        noise = np.random.default_rng([zlib.crc32(name.encode()), seed]).standard_normal(out[name].shape)
        drawn = base * np.exp(spread * noise) if base else spread * noise
        out[name] = jnp.asarray(drawn.astype(out[name].dtype))
    for name, factor in factors.items():
        out[name] = (out[name] * factor).astype(out[name].dtype)
    return out
```

```python
from contextlib import ExitStack

import numpy as np
import concourse.bass as bass
from concourse import mybir

ALU = mybir.AluOpType
ACT = mybir.ActivationFunctionType
F32 = mybir.dt.float32
I32 = mybir.dt.int32
AX = mybir.AxisListType

P = 128
D = 128
N = 3125
E = 100000
BLOCKS = -(-N // P)
ROWS = BLOCKS * P
TILES = -(-E // P)
EDGES = TILES * P
PAD_NODE = ROWS - 1
CHUNK = 5
CHUNKS = BLOCKS // CHUNK
CW = CHUNK * D
PAIRS = TILES + BLOCKS - 1
GROUP = 8
ROUNDS = -(-PAIRS // (2 * GROUP))
PAIRS_PAD = ROUNDS * 2 * GROUP
PAIR_BLOCKS = -(-PAIRS_PAD // P)
PAIR_COLS = PAIR_BLOCKS * P
HEADS = 4
HEAD = D // HEADS
EDGE_DIM = 32
AW = D + HEADS
RELATIONS = 9
RW = 2 * RELATIONS * D
REC = 4
SCAT = 17
SCAT_ROUNDS = TILES // (2 * SCAT)
BIG = 1.0e30
EPS = 1e-5
BANK = 512

assert BLOCKS % CHUNK == 0 and TILES % (2 * SCAT) == 0


class Memory:
    spent = []

    def __init__(self, nc, stack):
        self.nc, self.stack = nc, stack

    @classmethod
    def clear(cls, nc):
        nc.clear_and_free_semaphores(cls.spent)
        nc.all_engine_barrier()
        cls.spent = []

    def sb(self, name, shape, dt=F32):
        return self.stack.enter_context(self.nc.sbuf_tensor(name, shape, dt))

    def sem(self, name):
        s = self.nc.alloc_semaphore(name)
        Memory.spent.append(s)
        return s


class Chain:

    def __init__(self, eng, sem, start=0):
        self.eng, self.sem, self.start, self.n = eng, sem, start, 0

    def __call__(self, ins):
        self.n += 1
        ins.then_inc(self.sem, 1)
        self.eng.wait_ge(self.sem, self.start + self.n)


def pairs_of(ps, half, width):
    return [ps[:, (half * GROUP // 2 + j // 2) * BANK + (j % 2) * (BANK // 2):][:, 0:width] for j in range(GROUP)]


def load_and_record(nc, S, dram, x, src, dst, etype, weight, edge_attr):
    with ExitStack() as stack:
        m = Memory(nc, stack)
        raw = {k: m.sb("raw_" + k, [P, TILES], I32) for k in ("src", "dst", "next", "type")}
        wt = m.sb("raw_w", [P, TILES])
        falls = m.sb("falls", [P, TILES])
        nfall = m.sb("nfall", [P, 1])
        flag_f = m.sb("flag_f", [1, 1])
        filled, loaded, placed = m.sem("filled"), m.sem("loaded"), m.sem("placed")
        consts, packed, counted, summed, flagged, stored = (m.sem(n) for n in (
            "consts", "packed", "counted", "fall_sum", "flagged", "rec_stored"))
        order, moved = m.sem("rec_order"), m.sem("attr_moved")
        full = E // TILES
        rest = E - full * TILES
        nrest = N - (BLOCKS - 1) * P
        rec = S["rec"]
        block = stack.enter_context(nc.Block())

        @block.gpsimd
        def _(pool):
            pool.memset(S["ident"][:, :], 1.0).then_inc(consts, 1)
            pool.memset(S["strict"][:, :], 1.0).then_inc(consts, 1)
            pool.memset(S["ones"][:, :], 1.0).then_inc(consts, 1)
            pool.wait_ge(consts, 3)
            pool.affine_select(out=S["ident"][:, :], in_=S["ident"][:, :], compare_op=ALU.is_equal, fill=0.0,
                               base=0, pattern=[[-1, P]], channel_multiplier=1).then_inc(placed, 1)
            pool.affine_select(out=S["strict"][:, :], in_=S["strict"][:, :], compare_op=ALU.is_gt, fill=0.0,
                               base=0, pattern=[[1, P]], channel_multiplier=-1).then_inc(placed, 1)
            pool.iota(S["col"][:, :], pattern=[[1, P]], base=0, channel_multiplier=0,
                      allow_small_or_imprecise_dtypes=True).then_inc(placed, 1)
            pool.iota(S["part"][:, :], pattern=[[0, 1]], base=0, channel_multiplier=1,
                      allow_small_or_imprecise_dtypes=True).then_inc(placed, 1)
            pool.wait_ge(placed, 4)

        @block.sync
        def _(sp):
            sp.wait_ge(filled, 7)
            for k, a, off in (("src", src, 0), ("dst", dst, 0), ("type", etype, 0)):
                sp.dma_start(raw[k][0:full, :], a[0:full * TILES].rearrange("(p c) -> p c", c=TILES)).then_inc(loaded, 16)
                sp.dma_start(raw[k][full:full + 1, 0:rest],
                             a[full * TILES:E].rearrange("(p c) -> p c", p=1)).then_inc(loaded, 16)
            sp.dma_start(raw["next"][0:full, :], dst[1:full * TILES + 1].rearrange("(p c) -> p c", c=TILES)).then_inc(loaded, 16)
            sp.dma_start(raw["next"][full:full + 1, 0:rest - 1],
                         dst[full * TILES + 1:E].rearrange("(p c) -> p c", p=1)).then_inc(loaded, 16)
            sp.dma_start(wt[0:full, :], weight[0:full * TILES].rearrange("(p c) -> p c", c=TILES)).then_inc(loaded, 16)
            sp.dma_start(wt[full:full + 1, 0:rest], weight[full * TILES:E].rearrange("(p c) -> p c", p=1)).then_inc(loaded, 16)
            sp.dma_start(S["x"][:, 0:(BLOCKS - 1) * D].rearrange("p (b d) -> p b d", d=D),
                         x[0:(BLOCKS - 1) * P, :].rearrange("(b p) d -> p b d", p=P)).then_inc(loaded, 16)
            sp.dma_start(S["x"][0:nrest, (BLOCKS - 1) * D:], x[(BLOCKS - 1) * P:N, :]).then_inc(loaded, 16)
            sp.wait_ge(packed, REC)
            sp.dma_start(dram["rec_by_dst"].rearrange("(p c) r -> p (c r)", p=P), rec[:, :]).then_inc(stored, 16)
            sp.wait_ge(flagged, 1)
            sp.dma_start(dram["flag"], S["flag"][:, :]).then_inc(stored, 16)
            sp.wait_ge(stored, 32)

        @block.scalar
        def _(act):
            act.dma_start(dram["attr"][0:E, :].rearrange("(a n) d -> a (n d)", a=16),
                          edge_attr.rearrange("(a n) d -> a (n d)", a=16)).then_inc(moved, 16)
            act.wait_ge(filled, 7)
            act.dma_start(dram["attr"][E:EDGES, :], S["zero"][0:EDGES - E, 0:EDGE_DIM]).then_inc(moved, 16)
            act.wait_ge(moved, 32)

        @block.vector
        def _(dve):
            for k in ("src", "dst", "next"):
                dve.memset(raw[k][:, :], PAD_NODE).then_inc(filled, 1)
            dve.memset(raw["type"][:, :], 0).then_inc(filled, 1)
            dve.memset(wt[:, :], 0.0).then_inc(filled, 1)
            dve.memset(S["x"][:, (BLOCKS - 1) * D:], 0.0).then_inc(filled, 1)
            dve.memset(S["zero"][:, :], 0.0).then_inc(filled, 1)
            dve.wait_ge(loaded, 16 * 12)
            rv = rec[:, :].rearrange("p (c r) -> p c r", r=REC)
            for n, a in enumerate((raw["src"], raw["dst"], raw["type"], wt)):
                dve.tensor_copy(rv[:, :, n], a[:, :]).then_inc(packed, 1)
            link = Chain(dve, order)
            link(dve.tensor_tensor(falls[:, :], raw["dst"][:, :], raw["next"][:, :], ALU.is_gt))
            dve.tensor_reduce(nfall[:, :], falls[:, :], AX.X, ALU.add).then_inc(counted, 1)
            dve.wait_ge(summed, 1)
            link(dve.tensor_copy(flag_f[:, :], S["ps"][0:1, 0:1]))
            dve.tensor_copy(S["flag"][:, :], flag_f[:, :]).then_inc(flagged, 1)

        @block.tensor
        def _(pe):
            pe.wait_ge(counted, 1)
            pe.wait_ge(placed, 4)
            pe.matmul(S["ps"][:, 0:1], S["ones"][:, :], nfall[:, :], start=True, stop=True).then_inc(summed, 1)


def sort_by_key(nc, S, name, field, keys, shift):
    with ExitStack() as stack:
        m = Memory(nc, stack)
        key = m.sb(name + "_key", [P, TILES])
        key_i = m.sb(name + "_keyi", [P, TILES], I32)
        mask = m.sb(name + "_mask", [P, TILES])
        ones = m.sb(name + "_one", [P, TILES])
        rank = m.sb(name + "_rank", [P, TILES])
        at = m.sb(name + "_at", [P, TILES])
        posf = m.sb(name + "_posf", [P, TILES])
        k_now = m.sb(name + "_k", [P, 1])
        total = m.sb(name + "_total", [P, 1])
        first = m.sb(name + "_first", [P, 1])
        ranked, prefixed, order, again = (m.sem(name + n) for n in ("_ranked", "_prefixed", "_order", "_again"))
        rv = S["rec"][:, :].rearrange("p (c r) -> p c r", r=REC)
        STEPS = 5
        block = stack.enter_context(nc.Block())

        @block.vector
        def _(dve):
            link = Chain(dve, order)
            link(dve.memset(ones[:, :], 1.0))
            link(dve.memset(posf[:, :], 0.0))
            link(dve.memset(k_now[:, :], 0.0))
            link(dve.memset(total[:, :], -1.0))
            link(dve.tensor_copy(key_i[:, :], rv[:, :, field]))
            if shift:
                link(dve.tensor_scalar(key_i[:, :], key_i[:, :], shift, None, ALU.arith_shift_right))
            link(dve.tensor_copy(key[:, :], key_i[:, :]))
            done = link.n
            with dve.Fori(0, keys) as i:
                step = Chain(dve, order, i * STEPS + done)
                step(dve.tensor_scalar(mask[:, :], key[:, :], k_now[:, 0:1], None, ALU.is_equal))
                dve.tensor_tensor_scan(rank[:, :], ones[:, :], mask[:, :], 0.0, ALU.mult, ALU.add).then_inc(ranked, 1)
                dve.wait_ge(prefixed, i + 1)
                step(dve.tensor_tensor(first[:, :], S["ps"][:, 0:1], total[:, :], ALU.add))
                step(dve.tensor_tensor(total[:, :], S["ps"][:, 1:2], total[:, :], ALU.add))
                step(dve.scalar_tensor_tensor(at[:, :], rank[:, :], first[:, 0:1], mask[:, :], ALU.add, ALU.mult))
                step(dve.tensor_tensor(posf[:, :], posf[:, :], at[:, :], ALU.add))
                dve.tensor_scalar_add(k_now[:, :], k_now[:, :], 1.0).then_inc(again, 1)
                dve.wait_ge(again, i + 1)
                assert step.n == STEPS
            dve.tensor_copy(S["pos"][:, :], posf[:, :]).then_inc(again, 1)
            dve.wait_ge(again, keys + 1)

        @block.tensor
        def _(pe):
            with pe.Fori(0, keys) as i:
                pe.wait_ge(ranked, i + 1)
                last = rank[:, TILES - 1:TILES]
                pe.matmul(S["ps"][:, 0:1], S["strict"][:, :], last, start=True, stop=True)
                pe.matmul(S["ps"][:, 1:2], S["ones"][:, :], last, start=True, stop=True).then_inc(prefixed, 1)


def scatter_records(nc, S, name, target, attr_from=None, attr_to=None):
    with ExitStack() as stack:
        m = Memory(nc, stack)
        place = m.sb(name + "_place", [P, 2 * SCAT], I32)
        carry = m.sb(name + "_carry", [P, 2 * SCAT * REC])
        feats = m.sb(name + "_feats", [P, 2 * SCAT * EDGE_DIM]) if attr_from is not None else None
        copied = [m.sem(f"{name}_copied{h}") for h in range(2)]
        sent = [m.sem(f"{name}_sent{h}") for h in range(2)]
        fetched = [m.sem(f"{name}_fetched{h}") for h in range(2)]
        aside = m.sem(name + "_aside")
        per = SCAT * (2 if attr_from is not None else 1) * 16
        block = stack.enter_context(nc.Block())

        @block.gpsimd
        def _(pool):
            def one_round(i, again):
                for h in range(2):
                    if again:
                        pool.wait_ge(sent[h], i * per)
                        pool.nop(nofuse=True)
                    pool.tensor_copy(place[:, h * SCAT:(h + 1) * SCAT],
                                     S["pos"][:, bass.ds(i * (2 * SCAT) + h * SCAT, SCAT)]).then_inc(copied[h], 1)
                    pool.tensor_copy(carry[:, h * SCAT * REC:(h + 1) * SCAT * REC],
                                     S["rec"][:, bass.ds(i * (2 * SCAT * REC) + h * SCAT * REC, SCAT * REC)]).then_inc(copied[h], 1)
                    pool.wait_ge(copied[h], i * 2 + 2)
                    pool.nop(nofuse=True)
                    if attr_from is not None:
                        pool.wait_ge(fetched[h], i * 16 + 16)
                        pool.nop(nofuse=True)
                    for j in range(h * SCAT, (h + 1) * SCAT):
                        pool.indirect_dma_start(
                            out=target, out_offset=bass.IndirectOffsetOnAxis(ap=place[:, j:j + 1], axis=0),
                            in_=carry[:, j * REC:(j + 1) * REC], in_offset=None).then_inc(sent[h], 16)
                        if attr_from is not None:
                            pool.indirect_dma_start(
                                out=attr_to, out_offset=bass.IndirectOffsetOnAxis(ap=place[:, j:j + 1], axis=0),
                                in_=feats[:, j * EDGE_DIM:(j + 1) * EDGE_DIM], in_offset=None).then_inc(sent[h], 16)

            one_round(0, False)
            with pool.Fori(1, SCAT_ROUNDS) as i:
                one_round(i, True)
            for h in range(2):
                pool.wait_ge(sent[h], SCAT_ROUNDS * per)

        if attr_from is not None:
            @block.scalar
            def _(act):
                act.dma_start(attr_from.rearrange("(a n) d -> a (n d)", a=P), attr_to.rearrange("(a n) d -> a (n d)", a=P)).then_inc(aside, 16)

            @block.sync
            def _(sp):
                sp.wait_ge(aside, 16)
                whole = attr_from.rearrange("(p c) d -> p c d", p=P)

                def one_round(i, again):
                    for h in range(2):
                        if again:
                            sp.wait_ge(sent[h], i * per)
                        sp.dma_start(feats[:, h * SCAT * EDGE_DIM:(h + 1) * SCAT * EDGE_DIM].rearrange("p (c d) -> p c d", d=EDGE_DIM),
                                     whole[:, bass.ds(i * (2 * SCAT) + h * SCAT, SCAT), :]).then_inc(fetched[h], 16)

                one_round(0, False)
                with sp.Fori(1, SCAT_ROUNDS) as i:
                    one_round(i, True)


def staircase(nc, S, dram, name, records, node_field, outputs, rows_out=False):
    with ExitStack() as stack:
        m = Memory(nc, stack)
        rows = m.sb(name + "_rows", [P, PAIR_BLOCKS, P * REC])
        wide = m.sb(name + "_wide", [P, PAIR_BLOCKS, P])
        wide2 = m.sb(name + "_wide2", [P, PAIR_BLOCKS, P])
        below = m.sb(name + "_below", [P, TILES])
        count = m.sb(name + "_count", [P, BLOCKS - 1])
        count_i = m.sb(name + "_counti", [P, BLOCKS - 1], I32)
        first = m.sb(name + "_first", [P, BLOCKS - 1])
        pair = m.sb(name + "_pair", [P, PAIR_BLOCKS])
        bnum = m.sb(name + "_bnum", [P, BLOCKS - 1])
        past = m.sb(name + "_past", [P, PAIR_BLOCKS, BLOCKS - 1])
        blk = m.sb(name + "_blk", [P, PAIR_BLOCKS])
        base = m.sb(name + "_base", [P, PAIR_BLOCKS])
        dead = m.sb(name + "_dead", [P, PAIR_BLOCKS])
        tile = m.sb(name + "_tile", [P, PAIR_BLOCKS])
        tile_i = m.sb(name + "_tilei", [P, PAIR_BLOCKS], I32)
        steps = m.sb(name + "_columns", [P, 3 * PAIR_BLOCKS], I32)
        ready, counted, summed, tiled, got, stepped = (m.sem(name + n) for n in (
            "_iota", "_counted", "_sum", "_tiled", "_got", "_stepped"))
        order, built, turned, stored = (m.sem(name + n) for n in ("_order", "_built", "_turned", "_stored"))
        fields = rows[:, :, :].rearrange("p b (e r) -> p b e r", r=REC)
        block = stack.enter_context(nc.Block())
        n_rows = 2 if rows_out else 0

        @block.gpsimd
        def _(pool):
            pool.iota(pair[:, :], pattern=[[P, PAIR_BLOCKS]], base=0, channel_multiplier=1,
                      allow_small_or_imprecise_dtypes=True).then_inc(ready, 1)
            pool.iota(bnum[:, :], pattern=[[1, BLOCKS - 1]], base=1, channel_multiplier=0,
                      allow_small_or_imprecise_dtypes=True).then_inc(ready, 1)
            pool.wait_ge(tiled, 1)
            whole = records.rearrange("(t e) r -> t (e r)", e=P)
            for c in range(PAIR_BLOCKS):
                pool.indirect_dma_start(out=rows[:, c, :], out_offset=None, in_=whole,
                                        in_offset=bass.IndirectOffsetOnAxis(ap=tile_i[:, c:c + 1], axis=0)).then_inc(got, 16)

        @block.sync
        def _(sp):
            sp.wait_ge(stepped, 1)
            for k in range(3):
                sp.dma_start(dram["steps"][k, :].rearrange("(c p) -> p c", p=P),
                             steps[:, k * PAIR_BLOCKS:(k + 1) * PAIR_BLOCKS], allow_slow_non_contiguous=True).then_inc(stored, 16)
            sp.wait_ge(stored, 48)
            sp.dma_start(S[name + "_steps"][:, :], dram["steps"].rearrange("(a k) c -> a (k c)", a=1)).then_inc(stored, 16)
            if rows_out:
                sp.wait_ge(built, 1)
                sp.dma_start(dram["loc"].rearrange("(b p) e -> p b e", p=P), wide[:, :, :]).then_inc(stored, 16)
                sp.wait_ge(built, 2)
                sp.dma_start(dram["node"][1:1 + PAIR_COLS * P].rearrange("(b p e) -> p b e", p=P, e=P),
                             wide2[:, :, :]).then_inc(stored, 16)
            sp.wait_ge(stored, 64 + 16 * n_rows)

        @block.vector
        def _(dve):
            link = Chain(dve, order)
            nodes = S["rec"][:, :].rearrange("p (c r) -> p c r", r=REC)[:, :, node_field]
            for b in range(1, BLOCKS):
                link(dve.tensor_scalar(below[:, :], nodes, float(b * P), None, ALU.is_lt))
                link(dve.tensor_reduce(count[:, b - 1:b], below[:, :], AX.X, ALU.add))
            dve.engine_nop().then_inc(counted, 1)
            dve.wait_ge(summed, 1)
            link(dve.tensor_copy(count_i[:, :], S["ps"][:, 0:BLOCKS - 1]))
            link(dve.tensor_scalar(count_i[:, :], count_i[:, :], 7, None, ALU.arith_shift_right))
            link(dve.tensor_copy(first[:, :], count_i[:, :]))
            dve.wait_ge(ready, 2)
            link(dve.tensor_tensor(first[:, :], first[:, :], bnum[:, :], ALU.add))
            link(dve.tensor_tensor(past[:, :, :], pair[:, :].unsqueeze(2).to_broadcast([P, PAIR_BLOCKS, BLOCKS - 1]),
                                   first[:, :].unsqueeze(1).to_broadcast([P, PAIR_BLOCKS, BLOCKS - 1]), ALU.is_ge))
            link(dve.tensor_reduce(blk[:, :], past[:, :, :], AX.X, ALU.add))
            link(dve.tensor_tensor(tile[:, :], pair[:, :], blk[:, :], ALU.subtract))
            link(dve.tensor_scalar_min(tile[:, :], tile[:, :], float(TILES - 1)))
            dve.tensor_copy(tile_i[:, :], tile[:, :]).then_inc(tiled, 1)
            link(dve.tensor_scalar_mul(steps[:, 0:PAIR_BLOCKS], blk[:, :], float(AW)))
            link(dve.tensor_scalar_mul(steps[:, PAIR_BLOCKS:2 * PAIR_BLOCKS], blk[:, :], float(D)))
            link(dve.tensor_scalar_mul(steps[:, 2 * PAIR_BLOCKS:], tile[:, :], float(P)))
            dve.engine_nop().then_inc(stepped, 1)
            link(dve.tensor_scalar(dead[:, :], pair[:, :], float(PAIRS), float(8 * ROWS), ALU.is_ge, ALU.mult))
            link(dve.tensor_scalar_mul(base[:, :], blk[:, :], float(P)))
            link(dve.tensor_tensor(base[:, :], base[:, :], dead[:, :], ALU.add))
            dve.wait_ge(got, 16 * PAIR_BLOCKS)
            link(dve.tensor_tensor(wide[:, :, :], fields[:, :, :, node_field],
                                   base[:, :].unsqueeze(2).to_broadcast([P, PAIR_BLOCKS, P]), ALU.subtract))
            if rows_out:
                dve.engine_nop().then_inc(built, 1)
                dve.tensor_copy(wide2[:, :, :], fields[:, :, :, node_field]).then_inc(built, 1)
                dve.wait_ge(stored, 64 + 16 * n_rows)
            for n, (array, what) in enumerate([(S[name + "_loc"], None)] + outputs):
                if what is not None:
                    field, mult, add, cap = what
                    w = wide[:, :, :]
                    if field is None:
                        link(dve.tensor_copy(w, fields[:, :, :, add]))
                    else:
                        link(dve.tensor_scalar(w, fields[:, :, :, field], float(mult), float(add), ALU.mult, ALU.add))
                        if mult > 1:
                            link(dve.tensor_tensor(w, w, fields[:, :, :, 2], ALU.add))
                        if cap:
                            link(dve.tensor_scalar_min(w, w, float(cap)))
                dve.engine_nop().then_inc(built, 1)
                dve.wait_ge(turned, n + 1)
                link(dve.tensor_copy(array[:, :], S["ps"][:, 0:PAIR_COLS]))

        @block.tensor
        def _(pe):
            pe.wait_ge(counted, 1)
            pe.matmul(S["ps"][:, 0:BLOCKS - 1], S["ones"][:, :], count[:, :], start=True, stop=True).then_inc(summed, 1)
            for n in range(1 + len(outputs)):
                pe.wait_ge(built, n_rows + n + 1)
                for c in range(PAIR_BLOCKS):
                    last = pe.transpose(S["ps"][:, c * P:(c + 1) * P], wide[:, c, :], S["ident"][:, :])
                last.then_inc(turned, 1)


def load_columns(nc, S, eng, name, table, start):
    base = table * PAIR_COLS
    limits = [(BLOCKS - 1) * AW, (BLOCKS - 1) * D, (TILES - 1) * P]
    _, values = nc.values_load_multi_w_load_instructions(
        S[name + "_steps"][0:1, bass.ds(start + base, GROUP)], engines=[eng], min_val=0, max_val=limits[table],
        skip_runtime_bounds_check_because="counts of blocks and tiles, capped when they were made")
    return values


def gather_sum(nc, S, tag, name, table, index, weight=None, degree=False, fresh=True):
    width = AW if degree else D
    with ExitStack() as stack:
        m = Memory(nc, stack)
        got = m.sb(tag + "_got", [P, 2, GROUP, AW])
        hot = m.sb(tag + "_hot", [P, 2, GROUP, P])
        cur = m.sb(tag + "_cur", [P, 2 * GROUP], I32)
        landed, copied, summed, added, heated = ([m.sem(f"{tag}_{n}{h}") for h in range(2)] for n in (
            "landed", "copied", "summed", "added", "hot"))
        acc_order, hot_order, cleared = m.sem(tag + "_acc"), m.sem(tag + "_hot"), m.sem(tag + "_cleared")
        sums, loc = S["sums"], S[name + "_loc"]
        block = stack.enter_context(nc.Block())

        @block.gpsimd
        def _(pool):
            with pool.Fori(0, ROUNDS) as i:
                for h in range(2):
                    pool.wait_ge(summed[h], i + 1)
                    pool.nop(nofuse=True)
                    pool.tensor_copy(cur[:, h * GROUP:(h + 1) * GROUP],
                                     index[:, bass.ds(i * (2 * GROUP) + h * GROUP, GROUP)]).then_inc(copied[h], 1)
                    pool.wait_ge(copied[h], i + 1)
                    pool.nop(nofuse=True)
                    for j in range(GROUP):
                        c = h * GROUP + j
                        pool.indirect_dma_start(out=got[:, h, j, 0:D], out_offset=None, in_=table,
                                                in_offset=bass.IndirectOffsetOnAxis(ap=cur[:, c:c + 1], axis=0)).then_inc(landed[h], 16)

        @block.vector
        def _(dve):
            if fresh:
                dve.memset(sums[:, :], 0.0).then_inc(cleared, 1)
                dve.wait_ge(cleared, 1)
            if degree:
                dve.memset(got[:, :, :, D:AW], 1.0).then_inc(cleared, 1)
            dve.sem_inc(acc_order, 1)
            for h in range(2):
                dve.sem_inc(added[h], 1)
            with dve.Fori(0, ROUNDS) as i:
                columns = []
                for h in range(2):
                    start = i * (2 * GROUP) + h * GROUP
                    columns.append(load_columns(nc, S, mybir.EngineType.DVE, name, 0, start))
                    dve.wait_ge(summed[h], i + 1)
                    one = dve.tensor_tensor(hot[:, h], S["col"][:, :].unsqueeze(1).to_broadcast([P, GROUP, P]),
                                            loc[:, bass.ds(start, GROUP)].unsqueeze(2).to_broadcast([P, GROUP, P]), ALU.is_equal)
                    if weight is not None:
                        one.then_inc(hot_order, 1)
                        dve.wait_ge(hot_order, i * 2 + h + 1)
                        one = dve.tensor_tensor(hot[:, h], hot[:, h],
                                                weight[:, bass.ds(start, GROUP)].unsqueeze(2).to_broadcast([P, GROUP, P]), ALU.mult)
                    one.then_inc(heated[h], 1)
                for h in range(2):
                    dve.wait_ge(summed[h], i + 2)
                    for j, (part, col) in enumerate(zip(pairs_of(S["ps"], h, width), columns[h])):
                        dve.wait_ge(acc_order, i * (2 * GROUP) + h * GROUP + j + 1)
                        one = dve.tensor_tensor(sums[:, bass.ds(col, width)], sums[:, bass.ds(col, width)], part, ALU.add)
                        one.then_inc(acc_order, 1)
                    dve.wait_ge(acc_order, i * (2 * GROUP) + h * GROUP + GROUP + 1)
                    dve.sem_inc(added[h], 1)

        @block.tensor
        def _(pe):
            for h in range(2):
                pe.sem_inc(summed[h], 1)
            if fresh or degree:
                pe.wait_ge(cleared, int(fresh) + int(degree))
            with pe.Fori(0, ROUNDS) as i:
                for h in range(2):
                    pe.wait_ge(heated[h], i + 1)
                    pe.wait_ge(added[h], i + 1)
                    pe.wait_ge(landed[h], (i + 1) * (16 * GROUP))
                    for j, part in enumerate(pairs_of(S["ps"], h, width)):
                        last = pe.matmul(part, hot[:, h, j, :], got[:, h, j, 0:width], start=True, stop=True)
                    last.then_inc(summed[h], 1)


def layer_norm(dve, link, S, rooted, root_of, t, out_of):
    for b in range(CHUNK):
        last = dve.bn_stats(S["stats"][:, b, :], t[:, b * D:(b + 1) * D])
    link(last)
    dve.nop(nofuse=True)
    for b in range(CHUNK):
        last = dve.bn_aggr(S["moments"][:, b, :], S["stats"][:, b, :])
    link(last)
    dve.tensor_scalar_add(S["var"][:, :], S["moments"][:, :, 1], EPS).then_inc(S["var_ready"], 1)
    dve.wait_ge(rooted, root_of)
    link(dve.reciprocal(S["rstd"][:, :], S["root"][:, :]))
    for b in range(CHUNK):
        last = dve.tensor_scalar(out_of(b), t[:, b * D:(b + 1) * D], S["moments"][:, b, 0:1],
                                 S["rstd"][:, b:b + 1], ALU.subtract, ALU.mult)
    return last


def chunk_of(tensor, i, width=D):
    return tensor[:, bass.ds(i * (CHUNK * width), CHUNK * width)]


def load_weights(nc, S, dram, w):
    with ExitStack() as stack:
        m = Memory(nc, stack)
        raw = m.sb("raw_w12", [P, 2, D])
        blank, raw_in, in_place, turned, kept = m.sem("w_blank"), m.sem("raw_in"), m.sem("w_in_place"), m.sem("w_turned"), m.sem("w_kept")
        block = stack.enter_context(nc.Block())

        @block.sync
        def _(sp):
            sp.dma_start(raw[:, 0, :], w["L0_gnn_W1"]).then_inc(raw_in, 16)
            sp.dma_start(raw[:, 1, :], w["L0_gnn_W2"]).then_inc(raw_in, 16)
            n = 0
            for k, name in enumerate(("Wq", "Wk", "Wv", "Wskip")):
                sp.dma_start(S["w_qkvs"][:, k * D:(k + 1) * D], w["L1_gnn_" + name]).then_inc(in_place, 16)
                n += 1
            for k, name in enumerate(("W1", "W2")):
                sp.dma_start(S["w_l1"][:, k, :], w["L1_gnn_" + name]).then_inc(in_place, 16)
                n += 1
            sp.wait_ge(blank, 1)
            for g in range(P // EDGE_DIM):
                sp.dma_start(S["w_e"][g * EDGE_DIM:(g + 1) * EDGE_DIM, g * D:(g + 1) * D], w["L1_gnn_We"]).then_inc(in_place, 16)
                n += 1
            for k, name in enumerate(("L0_gnn_b1", "L1_gnn_b1")):
                sp.dma_start(S["b_col"][:, k:k + 1], w[name].rearrange("(p a) -> p a", a=1)).then_inc(in_place, 16)
                n += 1
            for k, name in enumerate(("L1_gnn_bq", "L1_gnn_bk", "L1_gnn_bv", "L1_gnn_bskip", "L0_gnn_b2", "L1_gnn_b2")):
                sp.dma_start(S["b_row"][:, k * D:(k + 1) * D],
                             w[name].rearrange("(a d) -> a d", a=1).to_broadcast([P, D])).then_inc(in_place, 16)
                n += 1
            sp.wait_ge(in_place, 16 * n)

        @block.tensor
        def _(pe):
            pe.wait_ge(raw_in, 32)
            for k in range(2):
                last = pe.transpose(S["ps"][:, k * D:(k + 1) * D], raw[:, k, :], S["ident"][:, :])
            last.then_inc(turned, 1)

        @block.vector
        def _(dve):
            dve.memset(S["w_e"][:, :], 0.0).then_inc(blank, 1)
            dve.wait_ge(turned, 1)
            dve.tensor_copy(S["w_l0"][:, :], S["ps"][:, 0:2 * D]).then_inc(kept, 1)
            dve.wait_ge(kept, 1)


def mlp_layer(nc, S, dram, tag, first):
    with ExitStack() as stack:
        m = Memory(nc, stack)
        den = m.sb(tag + "_den", [P, CHUNK, 1 if first else HEADS])
        agg = m.sb(tag + "_agg", [P, CW])
        agg_t = m.sb(tag + "_aggT", [P, CW])
        hid_t = m.sb(tag + "_hidT", [P, CW])
        t = m.sb(tag + "_t", [P, CW])
        t2 = m.sb(tag + "_t2", [P, CW])
        S["stats"] = m.sb(tag + "_stats", [P, CHUNK, 6])
        S["moments"] = m.sb(tag + "_moments", [P, CHUNK, 2])
        S["var"], S["root"], S["rstd"] = (m.sb(tag + n, [P, CHUNK]) for n in ("_var", "_root", "_rstd"))
        S["var_ready"] = m.sem(tag + "_varready")
        averaged, turned, kept, hidden, active, product, biased, gelued, rooted, order, normed, saved = (
            m.sem(f"{tag}_{n}") for n in ("averaged", "turned", "kept", "hidden", "active", "product", "biased",
                                          "gelued", "rooted", "order", "normed", "saved"))
        ps, half = S["ps"], CW // 2
        w1 = S["w_l0"][:, 0:D] if first else S["w_l1"][:, 0, :]
        w2 = S["w_l0"][:, D:2 * D] if first else S["w_l1"][:, 1, :]
        b1 = S["b_col"][:, 0:1] if first else S["b_col"][:, 1:2]
        b2 = S["b_row"][:, 4 * D:5 * D] if first else S["b_row"][:, 5 * D:6 * D]
        up = ps[:, 2 * BANK:4 * BANK].rearrange("p (a n) -> p a n", a=2)[:, :, 0:half]
        STEPS = 7 if first else 8
        block = stack.enter_context(nc.Block())

        @block.vector
        def _(dve):
            with dve.Fori(0, CHUNKS) as i:
                link = Chain(dve, order, i * STEPS)
                sums = chunk_of(S["sums"], i, AW).rearrange("p (b w) -> p b w", w=AW)
                x = chunk_of(S["x"], i)
                if first:
                    link(dve.tensor_scalar_max(den[:, :, 0], sums[:, :, D], 1.0))
                    link(dve.reciprocal(den[:, :, 0], den[:, :, 0]))
                    dve.tensor_tensor(agg[:, :].rearrange("p (b d) -> p b d", d=D), sums[:, :, 0:D],
                                      den[:, :, :].to_broadcast([P, CHUNK, D]), ALU.mult).then_inc(averaged, 1)
                else:
                    link(dve.tensor_scalar_add(den[:, :, :], sums[:, :, D:AW], 1e-16))
                    link(dve.reciprocal(den[:, :, :], den[:, :, :]))
                    link(dve.tensor_tensor(agg[:, :].rearrange("p (b h c) -> p b h c", h=HEADS, c=HEAD),
                                           sums[:, :, 0:D].rearrange("p b (h c) -> p b h c", c=HEAD),
                                           den[:, :, :].unsqueeze(3).to_broadcast([P, CHUNK, HEADS, HEAD]), ALU.mult))
                    dve.tensor_tensor(agg[:, :], agg[:, :], chunk_of(S["skip"], i), ALU.add).then_inc(averaged, 1)
                dve.wait_ge(product, i + 1)
                add = dve.tensor_tensor(t[:, :].rearrange("p (b d) -> p b d", d=D),
                                        ps[:, 4 * BANK:4 * BANK + CW].rearrange("p (b d) -> p b d", d=D),
                                        b2.unsqueeze(1).to_broadcast([P, CHUNK, D]), ALU.add)
                if first:
                    link(add)
                    link(dve.tensor_tensor(t[:, :], t[:, :], x, ALU.add))
                else:
                    add.then_inc(biased, 1)
                    dve.wait_ge(gelued, i + 1)
                    link(dve.tensor_tensor(t[:, :], t2[:, :], agg[:, :], ALU.add))
                    link(dve.tensor_tensor(t[:, :], t[:, :], x, ALU.add))
                last = layer_norm(dve, link, S, rooted, i + 1, t,
                                  lambda b: S["x"][:, bass.ds(i * CW + b * D, D)])
                last.then_inc(normed, 1)
                dve.wait_ge(normed, i + 1)
                assert link.n == STEPS, link.n

        @block.tensor
        def _(pe):
            with pe.Fori(0, CHUNKS) as i:
                pe.wait_ge(averaged, i + 1)
                for b in range(CHUNK):
                    last = pe.transpose(ps[:, b * D:(b + 1) * D], agg[:, b * D:(b + 1) * D], S["ident"][:, :])
                last.then_inc(turned, 1)
                pe.wait_ge(kept, i + 1)
                for a in range(2):
                    last = pe.matmul(up[:, a, :], w1, agg_t[:, a * half:(a + 1) * half], start=True, stop=True)
                last.then_inc(hidden, 1)
                pe.wait_ge(active, i + 1)
                for b in range(CHUNK):
                    last = pe.matmul(ps[:, 4 * BANK + b * D:4 * BANK + (b + 1) * D], hid_t[:, b * D:(b + 1) * D], w2,
                                     start=True, stop=True)
                last.then_inc(product, 1)

        @block.scalar
        def _(act):
            with act.Fori(0, CHUNKS) as i:
                act.wait_ge(turned, i + 1)
                act.activation(agg_t[:, :], ps[:, 0:CW], ACT.Copy).then_inc(kept, 1)
                act.wait_ge(hidden, i + 1)
                act.activation(hid_t[:, :].rearrange("p (a n) -> p a n", a=2), up,
                               ACT.Relu if first else ACT.Gelu_apprx_tanh, bias=b1).then_inc(active, 1)
                if not first:
                    act.wait_ge(biased, i + 1)
                    act.activation(t2[:, :], t[:, :], ACT.Gelu_apprx_tanh).then_inc(gelued, 1)
                act.wait_ge(S["var_ready"], i + 1)
                act.activation(S["root"][:, :], S["var"][:, :], ACT.Sqrt).then_inc(rooted, 1)

        if not first:
            @block.sync
            def _(sp):
                with sp.Fori(0, CHUNKS) as i:
                    sp.wait_ge(normed, i + 1)
                    sp.dma_start(dram["x2"][bass.ds(i * (CHUNK * P), CHUNK * P), :].rearrange("(b p) d -> p b d", p=P),
                                 chunk_of(S["x"], i).rearrange("p (b d) -> p b d", d=D)).then_inc(saved, 16)
                sp.wait_ge(saved, 16 * CHUNKS)


def project(nc, S, dram):
    with ExitStack() as stack:
        m = Memory(nc, stack)
        xs, x_t = m.sb("qkv_xs", [P, CW]), m.sb("qkv_xT", [P, CW])
        kv = m.sb("qkv_kv", [P, CHUNK, 2 * D])
        staged, turned, kept, product, split, saved = (m.sem("qkv_" + n) for n in (
            "staged", "turned", "kept", "product", "split", "saved"))
        ps = S["ps"]
        outs = ps[:, 2 * BANK:(2 + CHUNK) * BANK].rearrange("p (b n) -> p b n", b=CHUNK)
        block = stack.enter_context(nc.Block())

        @block.scalar
        def _(act):
            with act.Fori(0, CHUNKS) as i:
                act.wait_ge(split, i * 3 + 1)
                act.nop(nofuse=True)
                act.activation(xs[:, :], chunk_of(S["x"], i), ACT.Copy).then_inc(staged, 1)
                act.wait_ge(turned, i + 1)
                act.activation(x_t[:, :], ps[:, 0:CW], ACT.Copy).then_inc(kept, 1)

        @block.tensor
        def _(pe):
            with pe.Fori(0, CHUNKS) as i:
                pe.wait_ge(staged, i + 1)
                for b in range(CHUNK):
                    last = pe.transpose(ps[:, b * D:(b + 1) * D], xs[:, b * D:(b + 1) * D], S["ident"][:, :])
                last.then_inc(turned, 1)
                pe.wait_ge(kept, i + 1)
                for b in range(CHUNK):
                    last = pe.matmul(outs[:, b, :], x_t[:, b * D:(b + 1) * D], S["w_qkvs"][:, :], start=True, stop=True)
                last.then_inc(product, 1)

        @block.vector
        def _(dve):
            dve.sem_inc(split, 1)
            dve.sem_inc(saved, 16)
            with dve.Fori(0, CHUNKS) as i:
                dve.wait_ge(product, i + 1)
                for dest, lo, hi in ((chunk_of(S["q"], i).rearrange("p (b d) -> p b d", d=D), 0, D), (kv[:, :, :], D, 3 * D),
                                     (chunk_of(S["skip"], i).rearrange("p (b d) -> p b d", d=D), 3 * D, 4 * D)):
                    if hi - lo > D:
                        dve.wait_ge(saved, (i + 1) * 16)
                    dve.tensor_tensor(dest, outs[:, :, lo:hi],
                                      S["b_row"][:, lo:hi].unsqueeze(1).to_broadcast([P, CHUNK, hi - lo]), ALU.add).then_inc(split, 1)

        @block.sync
        def _(sp):
            with sp.Fori(0, CHUNKS) as i:
                sp.wait_ge(split, i * 3 + 4)
                sp.dma_start(dram["kv"][bass.ds(i * (CHUNK * P), CHUNK * P), :].rearrange("(b p) d -> p b d", p=P),
                             kv[:, :, :]).then_inc(saved, 16)
            sp.wait_ge(saved, 16 * (CHUNKS + 1))


def scores(nc, S, dram):
    HALF = GROUP // 2
    WHOLE = PAIRS_PAD // (2 * HALF)
    with ExitStack() as stack:
        m = Memory(nc, stack)
        kv = m.sb("sc_kv", [P, 2, HALF, 2 * D])
        kve = m.sb("sc_kve", [P, 2, HALF, 2 * D])
        attr = m.sb("sc_attr", [P, 2, HALF * EDGE_DIM])
        attr_t = m.sb("sc_attrT", [P, 2, P])
        locb = m.sb("sc_locb", [P, 2, HALF * P])
        hot_t = m.sb("sc_hotT", [P, 2, HALF * P])
        prod = m.sb("sc_prod", [P, 2, HALF * D])
        cur = m.sb("sc_cur", [P, 2 * HALF], I32)
        landed, copied, featured, placed, turned, kept, heated, product, added, multiplied, scored, saved = (
            [m.sem(f"sc_{n}{h}") for h in range(2)] for n in ("landed", "copied", "featured", "placed", "turned",
            "kept", "heated", "product", "added", "multiplied", "scored", "saved"))
        cleared = m.sem("sc_cleared")
        ps = S["ps"]
        block = stack.enter_context(nc.Block())

        def qe(h):
            return ps[:, h * 2 * BANK:h * 2 * BANK + HALF * D]

        def feat(h):
            return ps[:, h * 2 * BANK + BANK:h * 2 * BANK + BANK + HALF * D]

        @block.gpsimd
        def _(pool):
            with pool.Fori(0, WHOLE) as i:
                for h in range(2):
                    pool.wait_ge(added[h], i + 1)
                    pool.nop(nofuse=True)
                    pool.tensor_copy(cur[:, h * HALF:(h + 1) * HALF],
                                     S["d_src"][:, bass.ds(i * (2 * HALF) + h * HALF, HALF)]).then_inc(copied[h], 1)
                    pool.wait_ge(copied[h], i + 1)
                    pool.nop(nofuse=True)
                    for j in range(HALF):
                        c = h * HALF + j
                        pool.indirect_dma_start(out=kv[:, h, j, :], out_offset=None, in_=dram["kv"],
                                                in_offset=bass.IndirectOffsetOnAxis(ap=cur[:, c:c + 1], axis=0)).then_inc(landed[h], 16)

        @block.sync
        def _(sp):
            with sp.Fori(0, WHOLE) as i:
                for h in range(2):
                    start = i * (2 * HALF) + h * HALF
                    sp.wait_ge(turned[h], i + 1)
                    _, rows = nc.values_load_multi_w_load_instructions(
                        S["dst_steps"][0:1, bass.ds(start + 2 * PAIR_COLS, HALF)], engines=[mybir.EngineType.SP], min_val=0,
                        max_val=(TILES - 1) * P, skip_runtime_bounds_check_because="tile numbers capped when they were made")
                    for j in range(HALF):
                        sp.dma_start(attr[:, h, j * EDGE_DIM:(j + 1) * EDGE_DIM],
                                     dram["attr"][bass.ds(rows[j], P), :]).then_inc(featured[h], 16)
                    sp.wait_ge(heated[h], i + 1)
                    sp.dma_start(locb[:, h, :], dram["loc"][bass.ds(start, HALF), :].rearrange("(a k) e -> a (k e)", a=1)
                                 .to_broadcast([P, HALF * P])).then_inc(placed[h], 16)

        @block.scalar
        def _(act):
            for h in range(2):
                act.sem_inc(kept[h], 1)
                act.sem_inc(saved[h], 16)
            with act.Fori(0, WHOLE) as i:
                for h in range(2):
                    act.wait_ge(turned[h], i + 2)
                    act.wait_ge(product[h], i + 1)
                    act.activation(attr_t[:, h, :], ps[:, (4 + h) * BANK:(4 + h) * BANK + P], ACT.Copy).then_inc(kept[h], 1)
                for h in range(2):
                    act.wait_ge(added[h], i + 2)
                    act.dma_start(dram["ve"][bass.ds(i * (2 * HALF) + h * HALF, HALF), :, :].rearrange("k e d -> e k d"),
                                  kve[:, h, :, D:2 * D]).then_inc(saved[h], 16)
            for h in range(2):
                act.wait_ge(saved[h], 16 * (WHOLE + 1))

        @block.vector
        def _(dve):
            dve.memset(S["alpha"][:, :, :], 0.0).then_inc(cleared, 1)
            dve.wait_ge(cleared, 1)
            for h in range(2):
                for s in (heated, added, scored):
                    dve.sem_inc(s[h], 1)
            with dve.Fori(0, WHOLE) as i:
                for h in range(2):
                    dve.wait_ge(placed[h], (i + 1) * 16)
                    dve.wait_ge(product[h], i + 1)
                    dve.tensor_scalar(hot_t[:, h, :], locb[:, h, :], S["part"][:, 0:1], None, ALU.is_equal).then_inc(heated[h], 1)
                for h in range(2):
                    dve.wait_ge(landed[h], (i + 1) * (16 * HALF))
                    dve.wait_ge(product[h], i + 2)
                    dve.wait_ge(saved[h], (i + 1) * 16)
                    dve.tensor_tensor(kve[:, h].rearrange("p k (a d) -> p k a d", a=2), kv[:, h].rearrange("p k (a d) -> p k a d", a=2),
                                      feat(h).rearrange("p (k d) -> p k d", d=D).unsqueeze(2).to_broadcast([P, HALF, 2, D]),
                                      ALU.add).then_inc(added[h], 1)
                    dve.wait_ge(added[h], i + 2)
                    dve.tensor_tensor(prod[:, h, :].rearrange("p (k d) -> p k d", d=D), qe(h).rearrange("p (k d) -> p k d", d=D),
                                      kve[:, h, :, 0:D], ALU.mult).then_inc(multiplied[h], 1)
                    dve.wait_ge(multiplied[h], i + 1)
                    dve.tensor_reduce(S["alpha"][:, :, bass.ds(i * (2 * HALF) + h * HALF, HALF)].rearrange("p a k -> p k a"),
                                      prod[:, h, :].rearrange("p (k a c) -> p k a c", a=HEADS, c=HEAD), AX.X, ALU.add).then_inc(scored[h], 1)
                    dve.wait_ge(scored[h], i + 2)

        @block.tensor
        def _(pe):
            for h in range(2):
                pe.sem_inc(turned[h], 1)
                pe.sem_inc(product[h], 1)
            with pe.Fori(0, WHOLE) as i:
                for h in range(2):
                    pe.wait_ge(featured[h], (i + 1) * (16 * HALF))
                    pe.wait_ge(kept[h], i + 1)
                    pe.transpose(ps[:, (4 + h) * BANK:(4 + h) * BANK + P], attr[:, h, :], S["ident"][:, :]).then_inc(turned[h], 1)
                for h in range(2):
                    start = i * (2 * HALF) + h * HALF
                    _, cols = nc.values_load_multi_w_load_instructions(
                        S["dst_steps"][0:1, bass.ds(start + PAIR_COLS, HALF)], engines=[mybir.EngineType.PE], min_val=0,
                        max_val=(BLOCKS - 1) * D, skip_runtime_bounds_check_because="block numbers are counts of blocks")
                    pe.wait_ge(kept[h], i + 2)
                    pe.wait_ge(scored[h], i + 1)
                    pe.wait_ge(heated[h], i + 2)
                    pe.matmul(feat(h), attr_t[:, h, :], S["w_e"][:, :], start=True, stop=True)
                    for j in range(HALF):
                        last = pe.matmul(qe(h)[:, j * D:(j + 1) * D], hot_t[:, h, j * P:(j + 1) * P],
                                         S["q"][:, bass.ds(cols[j], D)], start=True, stop=True)
                    last.then_inc(product[h], 1)


def softmax_maxima(nc, S, dram):
    L = PAIRS_PAD
    HR = HEADS * PAIR_BLOCKS
    with ExitStack() as stack:
        m = Memory(nc, stack)
        turn = m.sb("mx_turn", [P, HR, P])
        node = m.sb("mx_node", [P, L])
        node_b = m.sb("mx_before", [P, L])
        node_a = m.sb("mx_after", [P, L])
        loc = m.sb("mx_loc", [P, L])
        bad = m.sb("mx_bad", [P, L])
        score = m.sb("mx_score", [P, HEADS, L])
        top = m.sb("mx_top", [P, HEADS, L])
        both = m.sb("mx_both", [P, L])
        ends = m.sb("mx_ends", [P, 2 * HEADS])
        anyc = m.sb("mx_any", [P, 1])
        over = m.sb("mx_over", [HEADS, 2, P])
        cross = m.sb("mx_cross", [HEADS, P + 1])
        into = m.sb("mx_into", [P, HEADS])
        front = m.sb("mx_front", [1, 1])
        turned, kept, stored, loaded, order, asked, told, ready, exped, done = (m.sem("mx_" + n) for n in (
            "turned", "kept", "stored", "loaded", "order", "asked", "told", "ready", "exped", "done"))
        fronted = m.sem("mx_fronted")
        ps = S["ps"]
        HALF_T = 14
        block = stack.enter_context(nc.Block())
        flat_alpha = dram["alpha"].rearrange("h b e -> h (b e)")
        flat_loc = dram["loc"].rearrange("b e -> (b e)")

        @block.tensor
        def _(pe):
            for n in range(HR):
                h, c = divmod(n, PAIR_BLOCKS)
                if n >= 4:
                    pe.wait_ge(kept, n - 3)
                pe.transpose(ps[:, (n % 4) * BANK:(n % 4) * BANK + P], S["alpha"][:, h, c * P:(c + 1) * P], S["ident"][:, :]).then_inc(turned, 1)
            for way in range(2):
                pe.wait_ge(asked, 2 * way + 1)
                pe.transpose(ps[0:HEADS, 4 * BANK:4 * BANK + P], ends[:, 0:HEADS], S["ident"][:, :])
                pe.transpose(ps[0:HEADS, 4 * BANK + P:4 * BANK + 2 * P], ends[:, HEADS:2 * HEADS], S["ident"][:, :]).then_inc(told, 1)
                pe.wait_ge(asked, 2 * way + 2)
                src = cross[:, 0:P] if way == 0 else cross[:, 1:P + 1]
                pe.transpose(ps[:, 5 * BANK:5 * BANK + HEADS], src, S["ident"][0:HEADS, 0:HEADS]).then_inc(told, 1)
            for n in range(HR):
                h, c = divmod(n, PAIR_BLOCKS)
                if n == 0:
                    pe.wait_ge(loaded, 16 * (4 + HEADS + HR))
                if n >= 4:
                    pe.wait_ge(done, n - 3)
                pe.transpose(ps[:, (n % 4) * BANK:(n % 4) * BANK + P], turn[:, n, :], S["ident"][:, :]).then_inc(turned, 1)

        @block.scalar
        def _(act):
            for n in range(HR):
                act.wait_ge(turned, n + 1)
                act.activation(turn[:, n, :], ps[:, (n % 4) * BANK:(n % 4) * BANK + P], ACT.Copy,
                               scale=float(HEAD) ** -0.5).then_inc(kept, 1)
            for h in range(HEADS):
                act.wait_ge(ready, h + 1)
                act.activation(score[:, h, :], score[:, h, :], ACT.Exp).then_inc(exped, 1)
            for n in range(HR):
                h, c = divmod(n, PAIR_BLOCKS)
                act.wait_ge(turned, HR + n + 1)
                act.activation(S["alpha"][:, h, c * P:(c + 1) * P], ps[:, (n % 4) * BANK:(n % 4) * BANK + P], ACT.Copy).then_inc(done, 1)
            act.wait_ge(done, HR)

        @block.sync
        def _(sp):
            sp.wait_ge(fronted, 1)
            sp.dma_start(dram["node"][0:1].rearrange("(a n) -> a n", a=1), front[:, :]).then_inc(stored, 16)
            for h in range(HEADS):
                sp.wait_ge(kept, (h + 1) * PAIR_BLOCKS)
                sp.dma_start(dram["alpha"][h].rearrange("(c p) e -> p c e", p=P),
                             turn[:, h * PAIR_BLOCKS:(h + 1) * PAIR_BLOCKS, :]).then_inc(stored, 16)
            sp.wait_ge(stored, 16 * (1 + HEADS))
            for t, a in ((node_b, dram["node"][0:P * L]), (node, dram["node"][1:1 + P * L]),
                         (node_a, dram["node"][2:2 + P * L]), (loc, flat_loc[0:P * L])):
                sp.dma_start(t[:, :], a.rearrange("(p c) -> p c", p=P)).then_inc(loaded, 16)
            for h in range(HEADS):
                sp.dma_start(score[:, h, :], flat_alpha[h, 0:P * L].rearrange("(p c) -> p c", p=P)).then_inc(loaded, 16)
            for h in range(HEADS):
                sp.wait_ge(exped, h + 1)
                sp.dma_start(flat_alpha[h, 0:P * L].rearrange("(p c) -> p c", p=P), score[:, h, :]).then_inc(stored, 16)
            sp.wait_ge(stored, 16 * (1 + 2 * HEADS))
            for h in range(HEADS):
                for c in range(PAIR_BLOCKS):
                    sp.dma_start(turn[:, h * PAIR_BLOCKS + c, :], dram["alpha"][h, c * P:(c + 1) * P, :]).then_inc(loaded, 16)

        @block.vector
        def _(dve):
            link = Chain(dve, order)
            dve.memset(front[:, :], -1.0).then_inc(fronted, 1)
            dve.wait_ge(loaded, 16 * (4 + HEADS))
            link(dve.tensor_scalar(bad[:, :], loc[:, :], 0.0, None, ALU.is_lt))
            link(dve.tensor_scalar(loc[:, :], loc[:, :], float(P), None, ALU.is_ge))
            link(dve.tensor_tensor(bad[:, :], bad[:, :], loc[:, :], ALU.add))
            for h in range(HEADS):
                link(dve.scalar_tensor_tensor(score[:, h, :], bad[:, :], -BIG, score[:, h, :], ALU.mult, ALU.add))
            link(dve.tensor_tensor(node_b[:, :], node_b[:, :], node[:, :], ALU.not_equal))
            link(dve.tensor_tensor(node_a[:, :], node_a[:, :], node[:, :], ALU.not_equal))
            for way, edge in enumerate((node_b, node_a)):
                link(dve.tensor_reduce(anyc[:, :], edge[:, :], AX.X, ALU.max))
                link(dve.tensor_scalar_mul(edge[:, :], edge[:, :], -BIG))
                link(dve.tensor_scalar_mul(ends[:, HEADS:2 * HEADS], anyc[:, :].to_broadcast([P, HEADS]), -BIG))
                src = score if way == 0 else top

                def run(a):
                    return a if way == 0 else a[:, ::-1]
                edge_last = L - 1 if way == 0 else 0
                for h in range(HEADS):
                    link(dve.tensor_tensor_scan(run(both[:, :]), run(edge[:, :]), run(src[:, h, :]), -BIG, ALU.add, ALU.max))
                    link(dve.tensor_copy(ends[:, h:h + 1], both[:, edge_last:edge_last + 1]))
                dve.engine_nop().then_inc(asked, 1)
                dve.wait_ge(told, 2 * way + 1)
                link(dve.tensor_copy(over[:, :, :], ps[0:HEADS, 4 * BANK:4 * BANK + 2 * P].rearrange("p (a n) -> p a n", a=2)))
                if way == 0:
                    link(dve.memset(cross[:, 0:1], -BIG))
                    link(dve.tensor_tensor_scan(cross[:, 1:P + 1], over[:, 1, :], over[:, 0, :], -BIG, ALU.add, ALU.max))
                else:
                    link(dve.memset(cross[:, P:P + 1], -BIG))
                    link(dve.tensor_tensor_scan(cross[:, 0:P][:, ::-1], over[:, 1, ::-1], over[:, 0, ::-1], -BIG, ALU.add, ALU.max))
                dve.engine_nop().then_inc(asked, 1)
                dve.wait_ge(told, 2 * way + 2)
                link(dve.tensor_copy(into[:, :], ps[:, 5 * BANK:5 * BANK + HEADS]))
                for h in range(HEADS):
                    dest = top[:, h, :] if way == 0 else both[:, :]
                    link(dve.tensor_tensor_scan(run(dest), run(edge[:, :]), run(src[:, h, :]), into[:, h:h + 1], ALU.add, ALU.max))
                    if way == 1:
                        link(dve.tensor_tensor(score[:, h, :], score[:, h, :], both[:, :], ALU.subtract))
                        dve.engine_nop().then_inc(ready, 1)


def weigh_values(nc, S, dram):
    with ExitStack() as stack:
        m = Memory(nc, stack)
        ve = m.sb("wv_ve", [P, 2, GROUP, D])
        pv = m.sb("wv_pv", [P, 2, GROUP, AW])
        hot = m.sb("wv_hot", [P, 2, GROUP, P])
        landed, weighed, summed, added = ([m.sem(f"wv_{n}{h}") for h in range(2)] for n in ("landed", "weighed", "summed", "added"))
        acc_order, cleared = m.sem("wv_acc"), m.sem("wv_cleared")
        sums = S["sums"]
        block = stack.enter_context(nc.Block())

        @block.sync
        def _(sp):
            with sp.Fori(0, ROUNDS) as i:
                for h in range(2):
                    sp.wait_ge(weighed[h], i * 3 + 1)
                    sp.dma_start(ve[:, h], dram["ve"][bass.ds(i * (2 * GROUP) + h * GROUP, GROUP), :, :]
                                 .rearrange("k e d -> e k d")).then_inc(landed[h], 16)

        @block.vector
        def _(dve):
            dve.memset(sums[:, :], 0.0).then_inc(cleared, 1)
            dve.wait_ge(cleared, 1)
            dve.sem_inc(acc_order, 1)
            for h in range(2):
                dve.sem_inc(added[h], 1)
                dve.sem_inc(weighed[h], 1)
            with dve.Fori(0, ROUNDS) as i:
                columns = []
                for h in range(2):
                    start = i * (2 * GROUP) + h * GROUP
                    columns.append(load_columns(nc, S, mybir.EngineType.DVE, "dst", 0, start))
                    probs = S["alpha"][:, :, bass.ds(start, GROUP)].rearrange("p a k -> p k a")
                    dve.wait_ge(summed[h], i + 1)
                    dve.tensor_tensor(hot[:, h], S["col"][:, :].unsqueeze(1).to_broadcast([P, GROUP, P]),
                                      S["dst_loc"][:, bass.ds(start, GROUP)].unsqueeze(2).to_broadcast([P, GROUP, P]),
                                      ALU.is_equal).then_inc(weighed[h], 1)
                    dve.tensor_copy(pv[:, h, :, D:AW], probs).then_inc(weighed[h], 1)
                    dve.wait_ge(landed[h], (i + 1) * 16)
                    dve.tensor_tensor(pv[:, h, :, 0:D].rearrange("p k (a c) -> p k a c", c=HEAD),
                                      ve[:, h].rearrange("p k (a c) -> p k a c", c=HEAD),
                                      probs.unsqueeze(3).to_broadcast([P, GROUP, HEADS, HEAD]), ALU.mult).then_inc(weighed[h], 1)
                for h in range(2):
                    dve.wait_ge(summed[h], i + 2)
                    for j, (part, col) in enumerate(zip(pairs_of(S["ps"], h, AW), columns[h])):
                        dve.wait_ge(acc_order, i * (2 * GROUP) + h * GROUP + j + 1)
                        dve.tensor_tensor(sums[:, bass.ds(col, AW)], sums[:, bass.ds(col, AW)], part, ALU.add).then_inc(acc_order, 1)
                    dve.wait_ge(acc_order, i * (2 * GROUP) + h * GROUP + GROUP + 1)
                    dve.sem_inc(added[h], 1)

        @block.tensor
        def _(pe):
            for h in range(2):
                pe.sem_inc(summed[h], 1)
            with pe.Fori(0, ROUNDS) as i:
                for h in range(2):
                    pe.wait_ge(weighed[h], i * 3 + 4)
                    pe.wait_ge(added[h], i + 1)
                    for j, part in enumerate(pairs_of(S["ps"], h, AW)):
                        last = pe.matmul(part, hot[:, h, j, :], pv[:, h, j, :], start=True, stop=True)
                    last.then_inc(summed[h], 1)


def residual_norm(nc, S, dram, tag, light, out=None):
    with ExitStack() as stack:
        m = Memory(nc, stack)
        t = m.sb(tag + "_t", [P, CW])
        S["stats"] = m.sb(tag + "_stats", [P, CHUNK, 6])
        S["moments"] = m.sb(tag + "_moments", [P, CHUNK, 2])
        S["var"], S["root"], S["rstd"] = (m.sb(tag + n, [P, CHUNK]) for n in ("_var", "_root", "_rstd"))
        S["var_ready"] = m.sem(tag + "_varready")
        rooted, order, normed, saved = (m.sem(f"{tag}_{n}") for n in ("rooted", "order", "normed", "saved"))
        STEPS = 5 if light else 4
        block = stack.enter_context(nc.Block())

        @block.vector
        def _(dve):
            tv = t[:, :].rearrange("p (b d) -> p b d", d=D)
            with dve.Fori(0, CHUNKS) as i:
                link = Chain(dve, order, i * STEPS)
                sums = chunk_of(S["sums"], i, AW).rearrange("p (b w) -> p b w", w=AW)[:, :, 0:D]
                x = chunk_of(S["x"], i).rearrange("p (b d) -> p b d", d=D)
                if light:
                    link(dve.scalar_tensor_tensor(tv, sums, 3.0, x, ALU.mult, ALU.add))
                    link(dve.scalar_tensor_tensor(tv, tv, 0.25, x, ALU.mult, ALU.add))
                else:
                    link(dve.tensor_tensor(tv, sums, x, ALU.add))
                last = layer_norm(dve, link, S, rooted, i + 1, t,
                                  lambda b: S["x"][:, bass.ds(i * CW + b * D, D)])
                last.then_inc(normed, 1)
                dve.wait_ge(normed, i + 1)
                assert link.n == STEPS, link.n

        @block.scalar
        def _(act):
            with act.Fori(0, CHUNKS) as i:
                act.wait_ge(S["var_ready"], i + 1)
                act.activation(S["root"][:, :], S["var"][:, :], ACT.Sqrt).then_inc(rooted, 1)

        if out is not None:
            @block.sync
            def _(sp):
                sp.wait_ge(normed, CHUNKS)
                whole = (BLOCKS - 1) * P
                sp.dma_start(out[0:whole, :].rearrange("(b p) d -> p b d", p=P),
                             S["x"][:, 0:(BLOCKS - 1) * D].rearrange("p (b d) -> p b d", d=D)).then_inc(saved, 16)
                sp.dma_start(out[whole:N, :], S["x"][0:N - whole, (BLOCKS - 1) * D:]).then_inc(saved, 16)
                sp.wait_ge(saved, 32)


def messages(nc, S, dram, weights, biases):
    PIECES = -(-RW // BANK)
    BUFS = PIECES
    with ExitStack() as stack:
        m = Memory(nc, stack)
        w = m.sb("ms_w", [P, RW])
        bias = m.sb("ms_b", [P, RW])
        xs, x_t = m.sb("ms_xs", [P, CW]), m.sb("ms_xT", [P, CW])
        y = m.sb("ms_y", [P, 2, RW])
        loaded, staged, turned, kept, product, biased = (m.sem("ms_" + n) for n in (
            "loaded", "staged", "turned", "kept", "product", "biased"))
        saved = [m.sem(f"ms_saved{k}") for k in range(2)]
        ps = S["ps"]
        last_layer = weights.shape[0] - 1
        block = stack.enter_context(nc.Block())

        @block.sync
        def _(sp):
            sp.dma_start(w[:, :].rearrange("p (r h) -> p r h", h=D), weights[last_layer].rearrange("r e h -> e r h")).then_inc(loaded, 16)
            sp.dma_start(bias[:, :], biases[last_layer].rearrange("(a r) h -> a (r h)", a=1).to_broadcast([P, RW])).then_inc(loaded, 16)
            for k in range(2):
                sp.sem_inc(saved[k], 16)
            with sp.Fori(0, BLOCKS // CHUNK) as i:
                for b in range(CHUNK):
                    sp.wait_ge(biased, i * (CHUNK * PIECES) + (b + 1) * PIECES + BUFS)
                    sp.dma_start(dram["y"][bass.ds(i * (CHUNK * P) + b * P, P), :], y[:, 0, :] if b % 2 == 0 else y[:, 1, :]).then_inc(saved[b % 2], 16)
            sp.wait_ge(saved[0], 16 * (1 + 3 * CHUNKS))
            sp.wait_ge(saved[1], 16 * (1 + 2 * CHUNKS))

        @block.scalar
        def _(act):
            with act.Fori(0, CHUNKS) as i:
                act.wait_ge(product, i * (CHUNK * PIECES) + 1)
                act.nop(nofuse=True)
                act.activation(xs[:, :], chunk_of(S["x"], i), ACT.Copy).then_inc(staged, 1)
                act.wait_ge(turned, i + 1)
                act.activation(x_t[:, :], ps[:, 0:CW], ACT.Copy).then_inc(kept, 1)

        @block.tensor
        def _(pe):
            pe.wait_ge(loaded, 32)
            pe.sem_inc(product, 1)
            with pe.Fori(0, CHUNKS) as i:
                pe.wait_ge(staged, i + 1)
                for b in range(CHUNK):
                    last = pe.transpose(ps[:, b * D:(b + 1) * D], xs[:, b * D:(b + 1) * D], S["ident"][:, :])
                last.then_inc(turned, 1)
                pe.wait_ge(kept, i + 1)
                for b in range(CHUNK):
                    for k in range(PIECES):
                        n = b * PIECES + k
                        cols = min(BANK, RW - k * BANK)
                        bank = 2 + n % BUFS
                        pe.wait_ge(biased, i * (CHUNK * PIECES) + n + 1)
                        pe.matmul(ps[:, bank * BANK:bank * BANK + cols], x_t[:, b * D:(b + 1) * D],
                                  w[:, k * BANK:k * BANK + cols], start=True, stop=True).then_inc(product, 1)

        @block.vector
        def _(dve):
            dve.sem_inc(biased, BUFS)
            dve.wait_ge(loaded, 32)
            with dve.Fori(0, CHUNKS) as i:
                for b in range(CHUNK):
                    before = i * 3 + b // 2 if b % 2 == 0 else i * 2 + b // 2
                    dve.wait_ge(saved[b % 2], (before + 1) * 16)
                    for k in range(PIECES):
                        n = b * PIECES + k
                        cols = min(BANK, RW - k * BANK)
                        bank = 2 + n % BUFS
                        dve.wait_ge(product, i * (CHUNK * PIECES) + n + 2)
                        dve.tensor_tensor(y[:, b % 2, k * BANK:k * BANK + cols], ps[:, bank * BANK:bank * BANK + cols],
                                          bias[:, k * BANK:k * BANK + cols], ALU.add).then_inc(biased, 1)


def gnn_kernel(nc, ins, out):
    def scratch(name, shape, dt=F32):
        return nc.dram_tensor(name, shape, dt, kind="Internal").ap()

    dram = {
        "rec_by_dst": scratch("rec_by_dst", [EDGES, REC]), "rec_by_src": scratch("rec_by_src", [EDGES, REC]),
        "attr": scratch("attr", [EDGES, EDGE_DIM]), "attr_given": scratch("attr_given", [EDGES, EDGE_DIM]), "flag": scratch("flag", [1, 1], I32),
        "steps": scratch("steps", [3, PAIR_COLS], I32), "loc": scratch("loc", [PAIR_COLS, P]),
        "node": scratch("node", [PAIR_COLS * P + P]), "kv": scratch("kv", [ROWS, 2 * D]),
        "ve": scratch("ve", [PAIRS_PAD, P, D]), "alpha": scratch("alpha", [HEADS, PAIR_COLS, P]),
        "x2": scratch("x2", [ROWS, D]), "y": scratch("y", [ROWS, RW]),
    }
    Memory.spent = []
    with ExitStack() as stack:
        m = Memory(nc, stack)
        S = {
            "ident": m.sb("ident", [P, P]), "strict": m.sb("strict", [P, P]), "ones": m.sb("ones", [P, P]),
            "col": m.sb("col", [P, P]), "part": m.sb("part", [P, 1]), "flag": m.sb("flag_i", [1, 1], I32),
            "x": m.sb("x_rows", [P, BLOCKS * D]), "sums": m.sb("sums", [P, BLOCKS * AW]),
            "src_loc": m.sb("src_loc", [P, PAIR_COLS]), "s_dst": m.sb("s_dst", [P, PAIR_COLS], I32),
            "s_w": m.sb("s_w", [P, PAIR_COLS]), "s_msg": m.sb("s_msg", [P, PAIR_COLS], I32),
            "dst_loc": m.sb("dst_loc", [P, PAIR_COLS]), "d_src": m.sb("d_src", [P, PAIR_COLS], I32),
            "d_msg": m.sb("d_msg", [P, PAIR_COLS], I32), "s_capped": m.sb("s_capped", [P, PAIR_COLS], I32),
            "src_steps": m.sb("src_steps", [1, 3 * PAIR_COLS], I32), "dst_steps": m.sb("dst_steps", [1, 3 * PAIR_COLS], I32),
            "w_l0": m.sb("w_l0", [P, 2 * D]), "w_qkvs": m.sb("w_qkvs", [P, 4 * D]), "w_l1": m.sb("w_l1", [P, 2, D]),
            "w_e": m.sb("w_e", [P, 4 * D]), "b_col": m.sb("b_col", [P, 2]), "b_row": m.sb("b_row", [P, 6 * D]),
            "ps": stack.enter_context(nc.psum_tensor("ps", [P, 8 * BANK], F32)),
        }
        with ExitStack() as edges:
            e = Memory(nc, edges)
            S["rec"] = e.sb("rec", [P, TILES * REC])
            S["pos"] = e.sb("pos", [P, TILES], I32)
            S["zero"] = e.sb("zero", [P, EDGE_DIM])
            load_and_record(nc, S, dram, ins["x"], ins["src"], ins["dst"], ins["edge_type_9"], ins["edge_weight"], ins["edge_attr_32"])
            load_weights(nc, S, dram, ins)
            sort_by_key(nc, S, "bysrc", 0, BLOCKS, 7)
            scatter_records(nc, S, "bysrc", dram["rec_by_src"])
            unsorted = nc.values_load(S["flag"][0:1, 0:1], min_val=0, max_val=EDGES)
            with nc.If(unsorted > 0):
                for eng in (nc.gpsimd, nc.scalar, nc.tensor, nc.vector, nc.sync):
                    eng.nop(nofuse=True)
                sort_by_key(nc, S, "bydst", 1, ROWS, 0)
                scatter_records(nc, S, "bydst", dram["rec_by_dst"], dram["attr_given"], dram["attr"])
            staircase(nc, S, dram, "dst", dram["rec_by_dst"], 1,
                      [(S["d_src"], (0, 1, 0, None)), (S["d_msg"], (0, 2 * RELATIONS, 0, None))], rows_out=True)
            staircase(nc, S, dram, "src", dram["rec_by_src"], 0,
                      [(S["s_dst"], (1, 1, 0, None)), (S["s_capped"], (1, 1, 0, N - 1)), (S["s_w"], (None, 1, 3, None)),
                       (S["s_msg"], (1, 2 * RELATIONS, RELATIONS, None))])
        gather_sum(nc, S, "g0", "src", ins["x"], S["s_capped"], degree=True)
        mlp_layer(nc, S, dram, "m0", True)
        Memory.clear(nc)
        with ExitStack() as layer:
            a = Memory(nc, layer)
            S["skip"] = a.sb("skip", [P, BLOCKS * D])
            S["alpha"] = a.sb("alpha_cols", [P, HEADS, PAIR_COLS])
            with ExitStack() as early:
                S["q"] = Memory(nc, early).sb("q", [P, BLOCKS * D])
                project(nc, S, dram)
                scores(nc, S, dram)
            softmax_maxima(nc, S, dram)
            weigh_values(nc, S, dram)
            mlp_layer(nc, S, dram, "m1", False)
        Memory.clear(nc)
        gather_sum(nc, S, "g2", "src", dram["x2"], S["s_dst"], weight=S["s_w"])
        residual_norm(nc, S, dram, "n2", True)
        messages(nc, S, dram, ins["L3_gnn_weights"], ins["L3_gnn_biases"])
        table = dram["y"].rearrange("n (r d) -> (n r) d", d=D)
        gather_sum(nc, S, "g3", "dst", table, S["d_msg"])
        gather_sum(nc, S, "g4", "src", table, S["s_msg"], fresh=False)
        residual_norm(nc, S, dram, "n3", False, out=out)


_INS = ["x", "src", "dst", "edge_attr_32", "edge_type_9", "edge_weight", "L0_gnn_W1", "L0_gnn_b1", "L0_gnn_W2", "L0_gnn_b2",
        "L1_gnn_Wq", "L1_gnn_bq", "L1_gnn_Wk", "L1_gnn_bk", "L1_gnn_Wv", "L1_gnn_bv", "L1_gnn_We", "L1_gnn_Wskip",
        "L1_gnn_bskip", "L1_gnn_W1", "L1_gnn_b1", "L1_gnn_W2", "L1_gnn_b2", "L3_gnn_weights", "L3_gnn_biases"]


def kernel(**inputs):
    import numpy as _np
    import concourse.bacc as _bacc
    from concourse import mybir as _mybir
    from concourse.bass_utils import run_bass_kernel_spmd as _run

    nc = _bacc.Bacc("TRN2", target_bir_lowering=False, num_devices=1)
    arrays, aps = {}, {}
    for name in _INS:
        a = _np.ascontiguousarray(inputs[name])
        arrays[f"in_{name}_dram"] = a
        aps[name] = nc.dram_tensor(f"in_{name}_dram", a.shape, _mybir.dt.from_np(a.dtype), kind="ExternalInput").ap()
    out = nc.dram_tensor("out_0_dram", (N, D), F32, kind="ExternalOutput").ap()
    gnn_kernel(nc, aps, out)
    r = _run(nc, [arrays], core_ids=[0])
    return r.results[0]["out_0_dram"]
```

```python
from contextlib import ExitStack

import numpy as np
import concourse.bass as bass
from concourse import mybir

ALU = mybir.AluOpType
ACT = mybir.ActivationFunctionType
F32 = mybir.dt.float32
I32 = mybir.dt.int32
AX = mybir.AxisListType

P = 128
D = 128
N = 3125
E = 100000
BLOCKS = -(-N // P)
ROWS = BLOCKS * P
TILES = -(-E // P)
EDGES = TILES * P
PAD_NODE = ROWS - 1
CHUNK = 5
CHUNKS = BLOCKS // CHUNK
CW = CHUNK * D
PAIRS = TILES + BLOCKS - 1
GROUP = 8
ROUNDS = -(-PAIRS // (2 * GROUP))
PAIRS_PAD = ROUNDS * 2 * GROUP
PAIR_BLOCKS = -(-PAIRS_PAD // P)
PAIR_COLS = PAIR_BLOCKS * P
HEADS = 4
HEAD = D // HEADS
EDGE_DIM = 32
AW = D + HEADS
RELATIONS = 9
RW = 2 * RELATIONS * D
REC = 5
MSG = D + 1 + 4
SCAT = 17
SCAT_ROUNDS = TILES // (2 * SCAT)
BIG = 1.0e30
NOWHERE = 2 * EDGES
EPS = 1e-5
BANK = 512

assert PAIRS_PAD % 24 == 0 and PAIRS_PAD + 2 * GROUP <= PAIR_COLS and BLOCKS % CHUNK == 0 and TILES % (2 * SCAT) == 0


class Memory:
    spent = []

    def __init__(self, nc, stack):
        self.nc, self.stack = nc, stack

    @classmethod
    def clear(cls, nc):
        nc.clear_and_free_semaphores(cls.spent)
        nc.all_engine_barrier()
        cls.spent = []

    def sb(self, name, shape, dt=F32):
        return self.stack.enter_context(self.nc.sbuf_tensor(name, shape, dt))

    def sem(self, name):
        s = self.nc.alloc_semaphore(name)
        Memory.spent.append(s)
        return s


class Chain:

    def __init__(self, eng, sem, start=0):
        self.eng, self.sem, self.start, self.n = eng, sem, start, 0

    def __call__(self, ins):
        self.n += 1
        ins.then_inc(self.sem, 1)
        self.eng.wait_ge(self.sem, self.start + self.n)


def pairs_of(ps, half, width):
    return [ps[:, (half * GROUP // 2 + j // 2) * BANK + (j % 2) * (BANK // 2):][:, 0:width] for j in range(GROUP)]


def load_and_record(nc, S, dram, x, src, dst, etype, weight, edge_attr):
    with ExitStack() as stack:
        m = Memory(nc, stack)
        raw = {k: m.sb("raw_" + k, [P, TILES], I32) for k in ("src", "dst", "next", "type")}
        wt = m.sb("raw_w", [P, TILES])
        falls = m.sb("falls", [P, TILES])
        nfall = m.sb("nfall", [P, 1])
        flag_f = m.sb("flag_f", [1, 1])
        filled, loaded, placed = m.sem("filled"), m.sem("loaded"), m.sem("placed")
        consts, packed, counted, summed, flagged = (m.sem(n) for n in (
            "consts", "packed", "counted", "fall_sum", "flagged"))
        order, moved = m.sem("rec_order"), S["attr_moved"]
        full = E // TILES
        rest = E - full * TILES
        nrest = N - (BLOCKS - 1) * P
        rec = S["rec"]
        block = stack.enter_context(nc.Block())

        @block.gpsimd
        def _(pool):
            pool.memset(S["ident"][:, :], 1.0).then_inc(consts, 1)
            pool.memset(S["strict"][:, :], 1.0).then_inc(consts, 1)
            pool.memset(S["ones"][:, :], 1.0).then_inc(consts, 1)
            pool.wait_ge(consts, 3)
            pool.affine_select(out=S["ident"][:, :], in_=S["ident"][:, :], compare_op=ALU.is_equal, fill=0.0,
                               base=0, pattern=[[-1, P]], channel_multiplier=1).then_inc(placed, 1)
            pool.affine_select(out=S["strict"][:, :], in_=S["strict"][:, :], compare_op=ALU.is_gt, fill=0.0,
                               base=0, pattern=[[1, P]], channel_multiplier=-1).then_inc(placed, 1)
            pool.iota(S["col"][:, :], pattern=[[1, P]], base=0, channel_multiplier=0,
                      allow_small_or_imprecise_dtypes=True).then_inc(placed, 1)
            pool.iota(S["part"][:, :], pattern=[[0, 1]], base=0, channel_multiplier=1,
                      allow_small_or_imprecise_dtypes=True).then_inc(placed, 1)
            pool.wait_ge(placed, 4)

        @block.sync
        def _(sp):
            sp.wait_ge(filled, 7)
            for k, a, off in (("src", src, 0), ("dst", dst, 0), ("type", etype, 0)):
                sp.dma_start(raw[k][0:full, :], a[0:full * TILES].rearrange("(p c) -> p c", c=TILES)).then_inc(loaded, 16)
                sp.dma_start(raw[k][full:full + 1, 0:rest],
                             a[full * TILES:E].rearrange("(p c) -> p c", p=1)).then_inc(loaded, 16)
            sp.dma_start(raw["next"][0:full, :], dst[1:full * TILES + 1].rearrange("(p c) -> p c", c=TILES)).then_inc(loaded, 16)
            sp.dma_start(raw["next"][full:full + 1, 0:rest - 1],
                         dst[full * TILES + 1:E].rearrange("(p c) -> p c", p=1)).then_inc(loaded, 16)
            sp.dma_start(wt[0:full, :], weight[0:full * TILES].rearrange("(p c) -> p c", c=TILES)).then_inc(loaded, 16)
            sp.dma_start(wt[full:full + 1, 0:rest], weight[full * TILES:E].rearrange("(p c) -> p c", p=1)).then_inc(loaded, 16)
            sp.dma_start(S["x"][:, 0:(BLOCKS - 1) * D].rearrange("p (b d) -> p b d", d=D),
                         x[0:(BLOCKS - 1) * P, :].rearrange("(b p) d -> p b d", p=P)).then_inc(loaded, 16)
            sp.dma_start(S["x"][0:nrest, (BLOCKS - 1) * D:], x[(BLOCKS - 1) * P:N, :]).then_inc(loaded, 16)

        @block.scalar
        def _(act):
            act.wait_ge(loaded, 16 * 12)
            act.dma_start(dram["attr"][0:E, :].rearrange("(a n) d -> a (n d)", a=16),
                          edge_attr.rearrange("(a n) d -> a (n d)", a=16)).then_inc(moved, 16)
            act.wait_ge(filled, 7)
            act.dma_start(dram["attr"][E:EDGES, :], S["zero"][0:EDGES - E, 0:EDGE_DIM]).then_inc(moved, 16)

        @block.vector
        def _(dve):
            for k in ("src", "dst", "next"):
                dve.memset(raw[k][:, :], PAD_NODE).then_inc(filled, 1)
            dve.memset(raw["type"][:, :], 0).then_inc(filled, 1)
            dve.memset(wt[:, :], 0.0).then_inc(filled, 1)
            dve.memset(S["x"][:, (BLOCKS - 1) * D:], 0.0).then_inc(filled, 1)
            dve.memset(S["zero"][:, :], 0.0).then_inc(filled, 1)
            dve.wait_ge(loaded, 16 * 12)
            rv = rec[:, :].rearrange("p (c r) -> p c r", r=REC)
            for n, a in enumerate((raw["src"], raw["dst"], raw["type"], wt)):
                dve.tensor_copy(rv[:, :, n], a[:, :]).then_inc(packed, 1)
            dve.memset(rv[:, :, REC - 1], 0.0).then_inc(packed, 1)
            link = Chain(dve, order)
            link(dve.tensor_tensor(falls[:, :], raw["dst"][:, :], raw["next"][:, :], ALU.is_gt))
            dve.tensor_reduce(nfall[:, :], falls[:, :], AX.X, ALU.add).then_inc(counted, 1)
            dve.wait_ge(summed, 1)
            link(dve.tensor_copy(flag_f[:, :], S["ps"][0:1, 0:1]))
            dve.tensor_copy(S["flag"][:, :], flag_f[:, :]).then_inc(flagged, 1)
            dve.wait_ge(flagged, 1)

        @block.tensor
        def _(pe):
            pe.wait_ge(counted, 1)
            pe.wait_ge(placed, 4)
            pe.matmul(S["ps"][:, 0:1], S["ones"][:, :], nfall[:, :], start=True, stop=True).then_inc(summed, 1)


def sort_by_key(nc, S, name, field, keys, shift):
    with ExitStack() as stack:
        m = Memory(nc, stack)
        key = m.sb(name + "_key", [P, TILES])
        key_i = m.sb(name + "_keyi", [P, TILES], I32)
        mask = m.sb(name + "_mask", [P, TILES])
        ones = m.sb(name + "_one", [P, TILES])
        rank = m.sb(name + "_rank", [P, TILES])
        at = m.sb(name + "_at", [P, TILES])
        posf = m.sb(name + "_posf", [P, TILES])
        k_now = m.sb(name + "_k", [P, 1])
        total = m.sb(name + "_total", [P, 1])
        first = m.sb(name + "_first", [P, 1])
        ranked, prefixed, order, again = (m.sem(name + n) for n in ("_ranked", "_prefixed", "_order", "_again"))
        rv = S["rec"][:, :].rearrange("p (c r) -> p c r", r=REC)
        STEPS = 5
        block = stack.enter_context(nc.Block())

        @block.vector
        def _(dve):
            link = Chain(dve, order)
            link(dve.memset(ones[:, :], 1.0))
            link(dve.memset(posf[:, :], 0.0))
            link(dve.memset(k_now[:, :], 0.0))
            link(dve.memset(total[:, :], -1.0))
            link(dve.tensor_copy(key_i[:, :], rv[:, :, field]))
            if shift:
                link(dve.tensor_scalar(key_i[:, :], key_i[:, :], shift, None, ALU.arith_shift_right))
            link(dve.tensor_copy(key[:, :], key_i[:, :]))
            done = link.n
            with dve.Fori(0, keys) as i:
                step = Chain(dve, order, i * STEPS + done)
                step(dve.tensor_scalar(mask[:, :], key[:, :], k_now[:, 0:1], None, ALU.is_equal))
                dve.tensor_tensor_scan(rank[:, :], ones[:, :], mask[:, :], 0.0, ALU.mult, ALU.add).then_inc(ranked, 1)
                dve.wait_ge(prefixed, i + 1)
                step(dve.tensor_tensor(first[:, :], S["ps"][:, 0:1], total[:, :], ALU.add))
                step(dve.tensor_tensor(total[:, :], S["ps"][:, 1:2], total[:, :], ALU.add))
                step(dve.scalar_tensor_tensor(at[:, :], rank[:, :], first[:, 0:1], mask[:, :], ALU.add, ALU.mult))
                step(dve.tensor_tensor(posf[:, :], posf[:, :], at[:, :], ALU.add))
                dve.tensor_scalar_add(k_now[:, :], k_now[:, :], 1.0).then_inc(again, 1)
                dve.wait_ge(again, i + 1)
                assert step.n == STEPS
            dve.tensor_copy(S["pos"][:, :], posf[:, :]).then_inc(again, 1)
            dve.tensor_copy(rv[:, :, REC - 1], posf[:, :]).then_inc(again, 1)
            dve.wait_ge(again, keys + 2)

        @block.tensor
        def _(pe):
            with pe.Fori(0, keys) as i:
                pe.wait_ge(ranked, i + 1)
                last = rank[:, TILES - 1:TILES]
                pe.matmul(S["ps"][:, 0:1], S["strict"][:, :], last, start=True, stop=True)
                pe.matmul(S["ps"][:, 1:2], S["ones"][:, :], last, start=True, stop=True).then_inc(prefixed, 1)


def scatter_records(nc, S, name, target, attr_from=None, attr_to=None):
    with ExitStack() as stack:
        m = Memory(nc, stack)
        place = m.sb(name + "_place", [P, 2 * SCAT], I32)
        carry = m.sb(name + "_carry", [P, 2 * SCAT * REC])
        feats = m.sb(name + "_feats", [P, 2 * SCAT * EDGE_DIM]) if attr_from is not None else None
        copied = [m.sem(f"{name}_copied{h}") for h in range(2)]
        sent = [m.sem(f"{name}_sent{h}") for h in range(2)]
        fetched = [m.sem(f"{name}_fetched{h}") for h in range(2)]
        aside = m.sem(name + "_aside")
        per = SCAT * (2 if attr_from is not None else 1) * 16
        block = stack.enter_context(nc.Block())

        @block.gpsimd
        def _(pool):
            def one_round(i, again):
                for h in range(2):
                    if again:
                        pool.wait_ge(sent[h], i * per)
                        pool.nop(nofuse=True)
                    pool.tensor_copy(place[:, h * SCAT:(h + 1) * SCAT],
                                     S["pos"][:, bass.ds(i * (2 * SCAT) + h * SCAT, SCAT)]).then_inc(copied[h], 1)
                    pool.tensor_copy(carry[:, h * SCAT * REC:(h + 1) * SCAT * REC],
                                     S["rec"][:, bass.ds(i * (2 * SCAT * REC) + h * SCAT * REC, SCAT * REC)]).then_inc(copied[h], 1)
                    pool.wait_ge(copied[h], i * 2 + 2)
                    pool.nop(nofuse=True)
                    if attr_from is not None:
                        pool.wait_ge(fetched[h], i * 16 + 16)
                        pool.nop(nofuse=True)
                    for j in range(h * SCAT, (h + 1) * SCAT):
                        pool.indirect_dma_start(
                            out=target, out_offset=bass.IndirectOffsetOnAxis(ap=place[:, j:j + 1], axis=0),
                            in_=carry[:, j * REC:(j + 1) * REC], in_offset=None).then_inc(sent[h], 16)
                        if attr_from is not None:
                            pool.indirect_dma_start(
                                out=attr_to, out_offset=bass.IndirectOffsetOnAxis(ap=place[:, j:j + 1], axis=0),
                                in_=feats[:, j * EDGE_DIM:(j + 1) * EDGE_DIM], in_offset=None).then_inc(sent[h], 16)

            one_round(0, False)
            with pool.Fori(1, SCAT_ROUNDS) as i:
                one_round(i, True)
            for h in range(2):
                pool.wait_ge(sent[h], SCAT_ROUNDS * per)

        if attr_from is not None:
            @block.scalar
            def _(act):
                act.wait_ge(S["attr_moved"], 32)
                act.dma_start(attr_from.rearrange("(a n) d -> a (n d)", a=P), attr_to.rearrange("(a n) d -> a (n d)", a=P)).then_inc(aside, 16)

            @block.sync
            def _(sp):
                sp.wait_ge(aside, 16)
                whole = attr_from.rearrange("(p c) d -> p c d", p=P)

                def one_round(i, again):
                    for h in range(2):
                        if again:
                            sp.wait_ge(sent[h], i * per)
                        sp.dma_start(feats[:, h * SCAT * EDGE_DIM:(h + 1) * SCAT * EDGE_DIM].rearrange("p (c d) -> p c d", d=EDGE_DIM),
                                     whole[:, bass.ds(i * (2 * SCAT) + h * SCAT, SCAT), :]).then_inc(fetched[h], 16)

                one_round(0, False)
                with sp.Fori(1, SCAT_ROUNDS) as i:
                    one_round(i, True)


def store_records(nc, S, dram, name, reload=False):
    with ExitStack() as stack:
        moved = Memory(nc, stack).sem(name + "_moved")
        block = stack.enter_context(nc.Block())

        @block.sync
        def _(sp):
            table = dram["rec_by_dst"].rearrange("(p c) r -> p (c r)", p=P)
            ends = (S["rec"][:, :], table) if reload else (table, S["rec"][:, :])
            sp.dma_start(*ends).then_inc(moved, 16)
            if not reload:
                sp.wait_ge(S["attr_moved"], 32)
                sp.wait_ge(S["w_in_place"], 16 * S["w_parts"])
            sp.wait_ge(moved, 16)


def staircase(nc, S, dram, name, node_field, records=None, outputs=()):
    rows_out = records is not None
    with ExitStack() as stack:
        m = Memory(nc, stack)
        if rows_out:
            rows = m.sb(name + "_rows", [P, PAIR_BLOCKS, P * REC])
            wide = m.sb(name + "_wide", [P, PAIR_BLOCKS, P])
            wide2 = m.sb(name + "_wide2", [P, PAIR_BLOCKS, P])
            fields = rows[:, :, :].rearrange("p b (e r) -> p b e r", r=REC)
        below = m.sb(name + "_below", [P, TILES])
        count = m.sb(name + "_count", [P, BLOCKS - 1])
        count_i = m.sb(name + "_counti", [P, BLOCKS - 1], I32)
        first = m.sb(name + "_first", [P, BLOCKS - 1])
        pair = m.sb(name + "_pair", [P, PAIR_BLOCKS])
        bnum = m.sb(name + "_bnum", [P, BLOCKS - 1])
        past = m.sb(name + "_past", [P, PAIR_BLOCKS, BLOCKS - 1])
        blk = m.sb(name + "_blk", [P, PAIR_BLOCKS])
        base = m.sb(name + "_base", [P, PAIR_BLOCKS])
        dead = m.sb(name + "_dead", [P, PAIR_BLOCKS])
        tile = m.sb(name + "_tile", [P, PAIR_BLOCKS])
        tile_i = m.sb(name + "_tilei", [P, PAIR_BLOCKS], I32)
        steps = m.sb(name + "_columns", [P, 3 * PAIR_BLOCKS], I32)
        ready, counted, summed, tiled, got, stepped = (m.sem(name + n) for n in (
            "_iota", "_counted", "_sum", "_tiled", "_got", "_stepped"))
        order, built, turned, stored = (m.sem(name + n) for n in ("_order", "_built", "_turned", "_stored"))
        block = stack.enter_context(nc.Block())

        @block.gpsimd
        def _(pool):
            pool.iota(pair[:, :], pattern=[[P, PAIR_BLOCKS]], base=0, channel_multiplier=1,
                      allow_small_or_imprecise_dtypes=True).then_inc(ready, 1)
            pool.iota(bnum[:, :], pattern=[[1, BLOCKS - 1]], base=1, channel_multiplier=0,
                      allow_small_or_imprecise_dtypes=True).then_inc(ready, 1)
            if rows_out:
                pool.wait_ge(tiled, 1)
                whole = records.rearrange("(t e) r -> t (e r)", e=P)
                for c in range(PAIR_BLOCKS):
                    pool.indirect_dma_start(out=rows[:, c, :], out_offset=None, in_=whole,
                                            in_offset=bass.IndirectOffsetOnAxis(ap=tile_i[:, c:c + 1], axis=0)).then_inc(got, 16)

        @block.sync
        def _(sp):
            sp.wait_ge(stepped, 1)
            for k in range(3):
                sp.dma_start(dram["steps"][k, :].rearrange("(c p) -> p c", p=P),
                             steps[:, k * PAIR_BLOCKS:(k + 1) * PAIR_BLOCKS], allow_slow_non_contiguous=True).then_inc(stored, 16)
            sp.wait_ge(stored, 48)
            sp.dma_start(S[name + "_steps"][:, :], dram["steps"].rearrange("(a k) c -> a (k c)", a=1)).then_inc(stored, 16)
            if rows_out:
                sp.wait_ge(built, 1)
                sp.dma_start(dram["loc"].rearrange("(b p) e -> p b e", p=P), wide[:, :, :]).then_inc(stored, 16)
                sp.wait_ge(built, 2)
                sp.dma_start(dram["node"][1:1 + PAIR_COLS * P].rearrange("(b p e) -> p b e", p=P, e=P),
                             wide2[:, :, :]).then_inc(stored, 16)
            else:
                sp.wait_ge(built, 1)
                sp.dma_start(dram["base"].rearrange("(c p) -> p c", p=P), base[:, :], allow_slow_non_contiguous=True).then_inc(stored, 16)
                sp.wait_ge(stored, 80)
                sp.dma_start(S["s_base"][:, :], dram["base"].rearrange("(a c) -> a c", a=1).to_broadcast([P, PAIR_COLS])).then_inc(stored, 16)
            sp.wait_ge(stored, 96)

        @block.vector
        def _(dve):
            link = Chain(dve, order)
            nodes = S["rec"][:, :].rearrange("p (c r) -> p c r", r=REC)[:, :, node_field]
            for b in range(1, BLOCKS):
                link(dve.tensor_scalar(below[:, :], nodes, float(b * P), None, ALU.is_lt))
                link(dve.tensor_reduce(count[:, b - 1:b], below[:, :], AX.X, ALU.add))
            dve.engine_nop().then_inc(counted, 1)
            dve.wait_ge(summed, 1)
            link(dve.tensor_copy(count_i[:, :], S["ps"][:, 0:BLOCKS - 1]))
            link(dve.tensor_scalar(count_i[:, :], count_i[:, :], 7, None, ALU.arith_shift_right))
            link(dve.tensor_copy(first[:, :], count_i[:, :]))
            dve.wait_ge(ready, 2)
            link(dve.tensor_tensor(first[:, :], first[:, :], bnum[:, :], ALU.add))
            link(dve.tensor_tensor(past[:, :, :], pair[:, :].unsqueeze(2).to_broadcast([P, PAIR_BLOCKS, BLOCKS - 1]),
                                   first[:, :].unsqueeze(1).to_broadcast([P, PAIR_BLOCKS, BLOCKS - 1]), ALU.is_ge))
            link(dve.tensor_reduce(blk[:, :], past[:, :, :], AX.X, ALU.add))
            link(dve.tensor_tensor(tile[:, :], pair[:, :], blk[:, :], ALU.subtract))
            link(dve.tensor_scalar_min(tile[:, :], tile[:, :], float(TILES - 1)))
            dve.tensor_copy(tile_i[:, :], tile[:, :]).then_inc(tiled, 1)
            link(dve.tensor_scalar_mul(steps[:, 0:PAIR_BLOCKS], blk[:, :], float(AW)))
            link(dve.tensor_scalar_mul(steps[:, PAIR_BLOCKS:2 * PAIR_BLOCKS], blk[:, :], float(D)))
            link(dve.tensor_scalar_mul(steps[:, 2 * PAIR_BLOCKS:], tile[:, :], float(P)))
            dve.engine_nop().then_inc(stepped, 1)
            link(dve.tensor_scalar(dead[:, :], pair[:, :], float(PAIRS), float(8 * ROWS), ALU.is_ge, ALU.mult))
            link(dve.tensor_scalar_mul(base[:, :], blk[:, :], float(P)))
            link(dve.tensor_tensor(base[:, :], base[:, :], dead[:, :], ALU.add))
            if not rows_out:
                dve.engine_nop().then_inc(built, 1)
                return
            dve.wait_ge(got, 16 * PAIR_BLOCKS)
            w = wide[:, :, :]
            link(dve.tensor_tensor(w, fields[:, :, :, node_field],
                                   base[:, :].unsqueeze(2).to_broadcast([P, PAIR_BLOCKS, P]), ALU.subtract))
            dve.engine_nop().then_inc(built, 1)
            dve.tensor_copy(wide2[:, :, :], fields[:, :, :, node_field]).then_inc(built, 1)
            dve.wait_ge(stored, 96)
            for n, (array, field, what) in enumerate([(S[name + "_loc"][:, :], node_field, "local")] + outputs):
                if what == "place":
                    link(dve.tensor_scalar(wide2[:, :, :], w, 0.0, float(NOWHERE), ALU.is_lt, ALU.mult))
                    link(dve.tensor_scalar(w, w, float(P), float(NOWHERE), ALU.is_ge, ALU.mult))
                    link(dve.tensor_tensor(w, w, wide2[:, :, :], ALU.add))
                    link(dve.tensor_tensor(w, w, fields[:, :, :, field], ALU.add))
                elif what == "message":
                    link(dve.scalar_tensor_tensor(w, fields[:, :, :, field], float(2 * RELATIONS), fields[:, :, :, 2], ALU.mult, ALU.add))
                elif what == "back":
                    link(dve.scalar_tensor_tensor(w, fields[:, :, :, field], float(2 * RELATIONS), fields[:, :, :, 2], ALU.mult, ALU.add))
                    link(dve.tensor_scalar_add(w, w, float(RELATIONS)))
                elif what == "copy":
                    link(dve.tensor_copy(w, fields[:, :, :, field]))
                dve.engine_nop().then_inc(built, 1)
                dve.wait_ge(turned, n + 1)
                link(dve.tensor_copy(array, S["ps"][:, 0:PAIR_COLS]))

        @block.tensor
        def _(pe):
            pe.wait_ge(counted, 1)
            pe.matmul(S["ps"][:, 0:BLOCKS - 1], S["ones"][:, :], count[:, :], start=True, stop=True).then_inc(summed, 1)
            for n in range(1 + len(outputs) if rows_out else 0):
                pe.wait_ge(built, n + 3)
                for c in range(PAIR_BLOCKS):
                    last = pe.transpose(S["ps"][:, c * P:(c + 1) * P], wide[:, c, :], S["ident"][:, :])
                last.then_inc(turned, 1)


def send_rows(nc, S, dram):
    STEP, WAYS = 4, 6
    LAG = WAYS // 2
    WHOLE = PAIRS_PAD // (WAYS * STEP)
    with ExitStack() as stack:
        m = Memory(nc, stack)
        locb = m.sb("sr_locb", [P, WAYS, STEP * P])
        hot_t = m.sb("sr_hotT", [P, WAYS, STEP * P])
        pay = m.sb("sr_pay", [P, WAYS, STEP, MSG])
        place = m.sb("sr_place", [P, WAYS * STEP], I32)
        placed, heated, picked, laid, freed, copied, sent = (
            [m.sem(f"sr_{n}{q}") for q in range(WAYS)] for n in ("placed", "heated", "picked", "laid", "freed", "copied", "sent"))
        counters = m.sem("sr_counters")
        ps = S["ps"]
        block = stack.enter_context(nc.Block())

        @block.sync
        def _(sp):
            with sp.Fori(0, WHOLE) as i:
                for q in range(WAYS):
                    sp.wait_ge(heated[q], i + 1)
                    sp.dma_start(locb[:, q, :], dram["loc"][bass.ds(i * (WAYS * STEP) + q * STEP, STEP), :]
                                 .rearrange("(a k) e -> a (k e)", a=1).to_broadcast([P, STEP * P])).then_inc(placed[q], 16)

        @block.vector
        def _(dve):
            dve.memset(pay[:, :, :, D:D + 1], 1.0).then_inc(counters, 1)
            for q in range(WAYS):
                dve.sem_inc(heated[q], 1)
            with dve.Fori(0, WHOLE) as i:
                for q in range(WAYS):
                    dve.wait_ge(placed[q], (i + 1) * 16)
                    dve.wait_ge(picked[q], i + 1)
                    dve.tensor_scalar(hot_t[:, q, :], locb[:, q, :], S["part"][:, 0:1], None, ALU.is_equal).then_inc(heated[q], 1)

        @block.tensor
        def _(pe):
            for q in range(WAYS):
                pe.sem_inc(picked[q], 1)
            with pe.Fori(0, WHOLE) as i:
                for q in range(WAYS):
                    _, cols = nc.values_load_multi_w_load_instructions(
                        S["dst_steps"][0:1, bass.ds(i * (WAYS * STEP) + q * STEP + PAIR_COLS, STEP)], engines=[mybir.EngineType.PE],
                        min_val=0, max_val=(BLOCKS - 1) * D, skip_runtime_bounds_check_because="block numbers are counts of blocks")
                    pe.wait_ge(heated[q], i + 2)
                    pe.wait_ge(laid[q], i * 2 + 1)
                    for j in range(STEP):
                        last = pe.matmul(ps[:, q * BANK + j * P:q * BANK + (j + 1) * P], hot_t[:, q, j * P:(j + 1) * P],
                                         S["x"][:, bass.ds(cols[j], D)], start=True, stop=True)
                    last.then_inc(picked[q], 1)

        @block.scalar
        def _(act):
            for q in range(WAYS):
                act.sem_inc(laid[q], 1)
            with act.Fori(0, WHOLE) as i:
                for q in range(WAYS):
                    act.wait_ge(freed[q], i + 1)
                    act.nop(nofuse=True)
                    act.activation(pay[:, q, :, D + 1:MSG], S["d_rec"][:, bass.ds(i * (WAYS * STEP) + q * STEP, STEP), :],
                                   ACT.Copy).then_inc(laid[q], 1)
                    act.wait_ge(picked[q], i + 2)
                    act.activation(pay[:, q, :, 0:D], ps[:, q * BANK:(q + 1) * BANK].rearrange("p (k d) -> p k d", d=D),
                                   ACT.Copy).then_inc(laid[q], 1)

        @block.gpsimd
        def _(pool):
            for q in range(LAG):
                pool.sem_inc(freed[q], 1)
            pool.wait_ge(counters, 1)

            def index(i, q):
                pool.tensor_copy(place[:, q * STEP:(q + 1) * STEP],
                                 S["d_place"][:, bass.ds(i * (WAYS * STEP) + q * STEP, STEP)]).then_inc(copied[q], 1)

            def one_round(i, again):
                for q in range(WAYS):
                    if q >= LAG:
                        pool.wait_ge(sent[q - LAG], i * (16 * STEP) + 16 * STEP)
                        pool.sem_inc(freed[q - LAG], 1)
                    else:
                        if again:
                            pool.wait_ge(sent[q + LAG], i * (16 * STEP))
                        pool.sem_inc(freed[q + LAG], 1)
                    if q + 1 < WAYS:
                        index(i, q + 1)
                    else:
                        index(i + 1, 0)
                    pool.wait_ge(copied[q], i + 1)
                    pool.wait_ge(laid[q], i * 2 + 3)
                    pool.nop(nofuse=True)
                    for j in range(STEP):
                        c = q * STEP + j
                        pool.indirect_dma_start(
                            out=dram["msg"], out_offset=bass.IndirectOffsetOnAxis(ap=place[:, c:c + 1], axis=0),
                            in_=pay[:, q, j, :], in_offset=None, bounds_check=EDGES - 1, oob_is_err=False).then_inc(sent[q], 16)

            index(0, 0)
            one_round(0, False)
            with pool.Fori(1, WHOLE) as i:
                one_round(i, True)
            for q in range(WAYS):
                pool.wait_ge(sent[q], WHOLE * 16 * STEP)


def first_sum(nc, S, dram):
    width = D + 1
    STEP, WAYS, SLOTS = 4, 6, 3
    WHOLE = PAIRS_PAD // (WAYS * STEP)
    with ExitStack() as stack:
        m = Memory(nc, stack)
        got = m.sb("fs_got", [P, WAYS, STEP, MSG])
        hot = m.sb("fs_hot", [P, WAYS, STEP, P])
        landed, summed, added, heated, noted, located = ([m.sem(f"fs_{n}{q}") for q in range(WAYS)] for n in (
            "landed", "summed", "added", "hot", "noted", "located"))
        acc_order = [m.sem(f"fs_acc{k}") for k in range(2)]
        cleared = m.sem("fs_cleared")
        sums = [S["sums"], m.sb("fs_odd", [P, BLOCKS * AW])]
        NOTES = 3
        block = stack.enter_context(nc.Block())

        def products(q):
            return [S["ps"][:, (q % SLOTS * 2 + j // 2) * BANK + (j % 2) * (BANK // 2):][:, 0:width] for j in range(STEP)]

        def fetch(eng, which, first):
            with eng.Fori(0, WHOLE) as i:
                for q in range(first, WAYS, 2):
                    _, rows = nc.values_load_multi_w_load_instructions(
                        S["src_steps"][0:1, bass.ds(i * (WAYS * STEP) + q * STEP + 2 * PAIR_COLS, STEP)], engines=[which],
                        min_val=0, max_val=(TILES - 1) * P, skip_runtime_bounds_check_because="tile numbers capped when they were made")
                    eng.wait_ge(summed[q], i + 1)
                    eng.wait_ge(noted[q], i * NOTES + 1)
                    for j in range(STEP):
                        eng.dma_start(got[:, q, j, :], dram["msg"][bass.ds(rows[j], P), :]).then_inc(landed[q], 16)

        @block.sync
        def _(sp):
            fetch(sp, mybir.EngineType.SP, 0)

        @block.scalar
        def _(act):
            fetch(act, mybir.EngineType.Activation, 1)

        @block.gpsimd
        def _(pool):
            for q in range(WAYS):
                pool.sem_inc(noted[q], 1)
            with pool.Fori(0, WHOLE) as i:
                for q in range(WAYS):
                    cols = bass.ds(i * (WAYS * STEP) + q * STEP, STEP)
                    pool.wait_ge(landed[q], (i + 1) * (16 * STEP))
                    pool.nop(nofuse=True)
                    for n, array in ((1, S["s_dst"]), (2, S["s_msg"]), (3, S["s_w"])):
                        pool.tensor_copy(array[:, cols], got[:, q, :, D + 1 + n]).then_inc(noted[q], 1)
            for q in range(WAYS):
                pool.wait_ge(noted[q], WHOLE * NOTES + 1)

        @block.vector
        def _(dve):
            for k in range(2):
                dve.memset(sums[k][:, :], 0.0).then_inc(cleared, 1)
            dve.wait_ge(cleared, 2)
            for k in range(2):
                dve.sem_inc(acc_order[k], 1)
            for q in range(WAYS):
                dve.sem_inc(added[q], 1)

            def heat(i, q):
                cols = bass.ds(i * (WAYS * STEP) + q * STEP, STEP)
                dve.wait_ge(landed[q], (i + 1) * (16 * STEP))
                dve.tensor_tensor(S["src_loc"][:, cols], got[:, q, :, D + 1], S["s_base"][:, cols], ALU.subtract).then_inc(located[q], 1)
                dve.wait_ge(located[q], i + 1)
                dve.wait_ge(summed[q], i + 1)
                dve.tensor_tensor(hot[:, q], S["col"][:, :].unsqueeze(1).to_broadcast([P, STEP, P]),
                                  S["src_loc"][:, cols].unsqueeze(2).to_broadcast([P, STEP, P]), ALU.is_equal).then_inc(heated[q], 1)

            def one_round(i, more):
                _, columns = nc.values_load_multi_w_load_instructions(
                    S["src_steps"][0:1, bass.ds(i * (WAYS * STEP), WAYS * STEP)], engines=[mybir.EngineType.DVE], min_val=0,
                    max_val=(BLOCKS - 1) * AW, skip_runtime_bounds_check_because="block numbers are counts of blocks")
                for q in range(WAYS):
                    if q + SLOTS < WAYS:
                        heat(i, q + SLOTS)
                    elif more:
                        heat(i + 1, q + SLOTS - WAYS)
                    dve.wait_ge(summed[q], i + 2)
                    for j, part in enumerate(products(q)):
                        k, n = j % 2, j // 2
                        col = columns[q * STEP + j]
                        dve.wait_ge(acc_order[k], i * (WAYS * STEP // 2) + q * (STEP // 2) + n + 1)
                        dve.tensor_tensor(sums[k][:, bass.ds(col, width)], sums[k][:, bass.ds(col, width)], part, ALU.add).then_inc(acc_order[k], 1)
                    for k in range(2):
                        dve.wait_ge(acc_order[k], i * (WAYS * STEP // 2) + (q + 1) * (STEP // 2) + 1)
                    dve.sem_inc(added[q], 1)

            for q in range(SLOTS):
                heat(0, q)
            with dve.Fori(0, WHOLE - 1) as i:
                one_round(i, True)
            one_round(WHOLE - 1, False)
            dve.tensor_tensor(sums[0][:, :], sums[0][:, :], sums[1][:, :], ALU.add).then_inc(cleared, 1)
            dve.wait_ge(cleared, 3)

        @block.tensor
        def _(pe):
            for q in range(WAYS):
                pe.sem_inc(summed[q], 1)
            with pe.Fori(0, WHOLE) as i:
                for q in range(WAYS):
                    pe.wait_ge(landed[q], (i + 1) * (16 * STEP))
                    if q < SLOTS:
                        pe.wait_ge(added[q + WAYS - SLOTS], i + 1)
                    else:
                        pe.wait_ge(added[q - SLOTS], i + 2)
                    pe.wait_ge(heated[q], i + 1)
                    for j, part in enumerate(products(q)):
                        last = pe.matmul(part, hot[:, q, j, :], got[:, q, j, 0:width], start=True, stop=True)
                    last.then_inc(summed[q], 1)


def load_columns(nc, S, eng, name, table, start):
    base = table * PAIR_COLS
    limits = [(BLOCKS - 1) * AW, (BLOCKS - 1) * D, (TILES - 1) * P]
    _, values = nc.values_load_multi_w_load_instructions(
        S[name + "_steps"][0:1, bass.ds(start + base, GROUP)], engines=[eng], min_val=0, max_val=limits[table],
        skip_runtime_bounds_check_because="counts of blocks and tiles, capped when they were made")
    return values


def gather_sum(nc, S, tag, name, table, index, weight=None, fresh=True):
    width = D
    with ExitStack() as stack:
        m = Memory(nc, stack)
        got = m.sb(tag + "_got", [P, 2, GROUP, D])
        hot = m.sb(tag + "_hot", [P, 2, GROUP, P])
        cur = m.sb(tag + "_cur", [P, 2 * GROUP], I32)
        landed, copied, summed, added, heated = ([m.sem(f"{tag}_{n}{h}") for h in range(2)] for n in (
            "landed", "copied", "summed", "added", "hot"))
        acc_order, hot_order, cleared = m.sem(tag + "_acc"), m.sem(tag + "_hot"), m.sem(tag + "_cleared")
        sums, loc = S["sums"], S[name + "_loc"]
        block = stack.enter_context(nc.Block())

        @block.gpsimd
        def _(pool):
            with pool.Fori(0, ROUNDS) as i:
                for h in range(2):
                    pool.wait_ge(summed[h], i + 1)
                    pool.nop(nofuse=True)
                    pool.tensor_copy(cur[:, h * GROUP:(h + 1) * GROUP],
                                     index[:, bass.ds(i * (2 * GROUP) + h * GROUP, GROUP)]).then_inc(copied[h], 1)
                    pool.wait_ge(copied[h], i + 1)
                    pool.nop(nofuse=True)
                    for j in range(GROUP):
                        c = h * GROUP + j
                        pool.indirect_dma_start(out=got[:, h, j, :], out_offset=None, in_=table,
                                                in_offset=bass.IndirectOffsetOnAxis(ap=cur[:, c:c + 1], axis=0)).then_inc(landed[h], 16)

        @block.vector
        def _(dve):
            if fresh:
                dve.memset(sums[:, :], 0.0).then_inc(cleared, 1)
                dve.wait_ge(cleared, 1)
            dve.sem_inc(acc_order, 1)
            for h in range(2):
                dve.sem_inc(added[h], 1)
            with dve.Fori(0, ROUNDS) as i:
                columns = []
                for h in range(2):
                    start = i * (2 * GROUP) + h * GROUP
                    columns.append(load_columns(nc, S, mybir.EngineType.DVE, name, 0, start))
                    dve.wait_ge(summed[h], i + 1)
                    one = dve.tensor_tensor(hot[:, h], S["col"][:, :].unsqueeze(1).to_broadcast([P, GROUP, P]),
                                            loc[:, bass.ds(start, GROUP)].unsqueeze(2).to_broadcast([P, GROUP, P]), ALU.is_equal)
                    if weight is not None:
                        one.then_inc(hot_order, 1)
                        dve.wait_ge(hot_order, i * 2 + h + 1)
                        one = dve.tensor_tensor(hot[:, h], hot[:, h],
                                                weight[:, bass.ds(start, GROUP)].unsqueeze(2).to_broadcast([P, GROUP, P]), ALU.mult)
                    one.then_inc(heated[h], 1)
                for h in range(2):
                    dve.wait_ge(summed[h], i + 2)
                    for j, (part, col) in enumerate(zip(pairs_of(S["ps"], h, width), columns[h])):
                        dve.wait_ge(acc_order, i * (2 * GROUP) + h * GROUP + j + 1)
                        one = dve.tensor_tensor(sums[:, bass.ds(col, width)], sums[:, bass.ds(col, width)], part, ALU.add)
                        one.then_inc(acc_order, 1)
                    dve.wait_ge(acc_order, i * (2 * GROUP) + h * GROUP + GROUP + 1)
                    dve.sem_inc(added[h], 1)

        @block.tensor
        def _(pe):
            for h in range(2):
                pe.sem_inc(summed[h], 1)
            with pe.Fori(0, ROUNDS) as i:
                for h in range(2):
                    pe.wait_ge(heated[h], i + 1)
                    pe.wait_ge(added[h], i + 1)
                    pe.wait_ge(landed[h], (i + 1) * (16 * GROUP))
                    for j, part in enumerate(pairs_of(S["ps"], h, width)):
                        last = pe.matmul(part, hot[:, h, j, :], got[:, h, j, 0:width], start=True, stop=True)
                    last.then_inc(summed[h], 1)


def layer_norm(dve, link, S, rooted, root_of, t, out_of):
    for b in range(CHUNK):
        last = dve.bn_stats(S["stats"][:, b, :], t[:, b * D:(b + 1) * D])
    link(last)
    dve.nop(nofuse=True)
    for b in range(CHUNK):
        last = dve.bn_aggr(S["moments"][:, b, :], S["stats"][:, b, :])
    link(last)
    dve.tensor_scalar_add(S["var"][:, :], S["moments"][:, :, 1], EPS).then_inc(S["var_ready"], 1)
    dve.wait_ge(rooted, root_of)
    link(dve.reciprocal(S["rstd"][:, :], S["root"][:, :]))
    for b in range(CHUNK):
        last = dve.tensor_scalar(out_of(b), t[:, b * D:(b + 1) * D], S["moments"][:, b, 0:1],
                                 S["rstd"][:, b:b + 1], ALU.subtract, ALU.mult)
    return last


def chunk_of(tensor, i, width=D):
    return tensor[:, bass.ds(i * (CHUNK * width), CHUNK * width)]


def load_weights(nc, S, dram, w):
    with ExitStack() as stack:
        m = Memory(nc, stack)
        raw = m.sb("raw_w12", [P, 2, D])
        blank, raw_in, in_place, turned, kept = m.sem("w_blank"), m.sem("raw_in"), S["w_in_place"], m.sem("w_turned"), m.sem("w_kept")
        block = stack.enter_context(nc.Block())

        @block.sync
        def _(sp):
            sp.dma_start(raw[:, 0, :], w["L0_gnn_W1"]).then_inc(raw_in, 16)
            sp.dma_start(raw[:, 1, :], w["L0_gnn_W2"]).then_inc(raw_in, 16)
            n = 0
            for k, name in enumerate(("Wq", "Wk", "Wv", "Wskip")):
                sp.dma_start(S["w_qkvs"][:, k * D:(k + 1) * D], w["L1_gnn_" + name]).then_inc(in_place, 16)
                n += 1
            for k, name in enumerate(("W1", "W2")):
                sp.dma_start(S["w_l1"][:, k, :], w["L1_gnn_" + name]).then_inc(in_place, 16)
                n += 1
            sp.wait_ge(blank, 1)
            for g in range(P // EDGE_DIM):
                sp.dma_start(S["w_e"][g * EDGE_DIM:(g + 1) * EDGE_DIM, g * D:(g + 1) * D], w["L1_gnn_We"]).then_inc(in_place, 16)
                n += 1
            for k, name in enumerate(("L0_gnn_b1", "L1_gnn_b1")):
                sp.dma_start(S["b_col"][:, k:k + 1], w[name].rearrange("(p a) -> p a", a=1)).then_inc(in_place, 16)
                n += 1
            for k, name in enumerate(("L1_gnn_bq", "L1_gnn_bk", "L1_gnn_bv", "L1_gnn_bskip", "L0_gnn_b2", "L1_gnn_b2")):
                sp.dma_start(S["b_row"][:, k * D:(k + 1) * D],
                             w[name].rearrange("(a d) -> a d", a=1).to_broadcast([P, D])).then_inc(in_place, 16)
                n += 1
            S["w_parts"] = n

        @block.tensor
        def _(pe):
            pe.wait_ge(raw_in, 32)
            for k in range(2):
                last = pe.transpose(S["ps"][:, k * D:(k + 1) * D], raw[:, k, :], S["ident"][:, :])
            last.then_inc(turned, 1)

        @block.vector
        def _(dve):
            dve.memset(S["w_e"][:, :], 0.0).then_inc(blank, 1)
            dve.wait_ge(turned, 1)
            dve.tensor_copy(S["w_l0"][:, :], S["ps"][:, 0:2 * D]).then_inc(kept, 1)
            dve.wait_ge(kept, 1)


def mlp_layer(nc, S, dram, tag, first):
    with ExitStack() as stack:
        m = Memory(nc, stack)
        den = m.sb(tag + "_den", [P, CHUNK, 1 if first else HEADS])
        agg = m.sb(tag + "_agg", [P, 2, CW])
        agg_t = m.sb(tag + "_aggT", [P, 2, CW])
        hid_t = m.sb(tag + "_hidT", [P, 2, CW])
        t = m.sb(tag + "_t", [P, CW])
        t2 = m.sb(tag + "_t2", [P, CW])
        S["stats"] = m.sb(tag + "_stats", [P, CHUNK, 6])
        S["moments"] = m.sb(tag + "_moments", [P, CHUNK, 2])
        S["var"], S["root"], S["rstd"] = (m.sb(tag + n, [P, CHUNK]) for n in ("_var", "_root", "_rstd"))
        S["var_ready"] = m.sem(tag + "_varready")
        averaged, turned, kept, hidden, active, product, biased, gelued, rooted, order, normed, saved = (
            m.sem(f"{tag}_{n}") for n in ("averaged", "turned", "kept", "hidden", "active", "product", "biased",
                                          "gelued", "rooted", "order", "normed", "saved"))
        ps, half = S["ps"], CW // 2
        w1 = S["w_l0"][:, 0:D] if first else S["w_l1"][:, 0, :]
        w2 = S["w_l0"][:, D:2 * D] if first else S["w_l1"][:, 1, :]
        b1 = S["b_col"][:, 0:1] if first else S["b_col"][:, 1:2]
        b2 = S["b_row"][:, 4 * D:5 * D] if first else S["b_row"][:, 5 * D:6 * D]
        up = ps[:, 2 * BANK:4 * BANK].rearrange("p (a n) -> p a n", a=2)[:, :, 0:half]
        block = stack.enter_context(nc.Block())

        @block.vector
        def _(dve):
            link = Chain(dve, order)

            def average(c):
                sums = S["sums"][:, c * CHUNK * AW:(c + 1) * CHUNK * AW].rearrange("p (b w) -> p b w", w=AW)
                a = agg[:, c % 2, :]
                if c:
                    dve.wait_ge(averaged, c)
                if c >= 2:
                    dve.wait_ge(turned, c - 1)
                if first:
                    link(dve.tensor_scalar_max(den[:, :, 0], sums[:, :, D], 1.0))
                    link(dve.reciprocal(den[:, :, 0], den[:, :, 0]))
                    dve.tensor_tensor(a.rearrange("p (b d) -> p b d", d=D), sums[:, :, 0:D],
                                      den[:, :, :].to_broadcast([P, CHUNK, D]), ALU.mult).then_inc(averaged, 1)
                else:
                    link(dve.tensor_scalar_add(den[:, :, :], sums[:, :, D:AW], 1e-16))
                    link(dve.reciprocal(den[:, :, :], den[:, :, :]))
                    link(dve.tensor_tensor(a.rearrange("p (b h c) -> p b h c", h=HEADS, c=HEAD),
                                           sums[:, :, 0:D].rearrange("p b (h c) -> p b h c", c=HEAD),
                                           den[:, :, :].unsqueeze(3).to_broadcast([P, CHUNK, HEADS, HEAD]), ALU.mult))
                    dve.tensor_tensor(a, a, S["skip"][:, c * CW:(c + 1) * CW], ALU.add).then_inc(averaged, 1)

            average(0)
            for c in range(CHUNKS):
                if c + 1 < CHUNKS:
                    average(c + 1)
                x = S["x"][:, c * CW:(c + 1) * CW]
                dve.wait_ge(product, c + 1)
                dve.tensor_tensor(t[:, :].rearrange("p (b d) -> p b d", d=D),
                                  ps[:, 4 * BANK:4 * BANK + CW].rearrange("p (b d) -> p b d", d=D),
                                  b2.unsqueeze(1).to_broadcast([P, CHUNK, D]), ALU.add).then_inc(biased, 1)
                if first:
                    dve.wait_ge(biased, c + 1)
                else:
                    dve.wait_ge(gelued, c + 1)
                    dve.wait_ge(averaged, c + 1)
                    link(dve.tensor_tensor(t[:, :], t2[:, :], agg[:, c % 2, :], ALU.add))
                link(dve.tensor_tensor(t[:, :], t[:, :], x, ALU.add))
                layer_norm(dve, link, S, rooted, c + 1, t,
                           lambda b: S["x"][:, c * CW + b * D:c * CW + (b + 1) * D]).then_inc(normed, 1)
                dve.wait_ge(normed, c + 1)

        @block.tensor
        def _(pe):
            def turn(c):
                pe.wait_ge(averaged, c + 1)
                for b in range(CHUNK):
                    last = pe.transpose(ps[:, b * D:(b + 1) * D], agg[:, c % 2, b * D:(b + 1) * D], S["ident"][:, :])
                last.then_inc(turned, 1)

            turn(0)
            for c in range(CHUNKS):
                pe.wait_ge(kept, c + 1)
                for a in range(2):
                    last = pe.matmul(up[:, a, :], w1, agg_t[:, c % 2, a * half:(a + 1) * half], start=True, stop=True)
                last.then_inc(hidden, 1)
                if c + 1 < CHUNKS:
                    turn(c + 1)
                pe.wait_ge(active, c + 1)
                if c:
                    pe.wait_ge(biased, c)
                for b in range(CHUNK):
                    last = pe.matmul(ps[:, 4 * BANK + b * D:4 * BANK + (b + 1) * D], hid_t[:, c % 2, b * D:(b + 1) * D], w2,
                                     start=True, stop=True)
                last.then_inc(product, 1)

        @block.scalar
        def _(act):
            def keep(c):
                act.wait_ge(turned, c + 1)
                act.activation(agg_t[:, c % 2, :], ps[:, 0:CW], ACT.Copy).then_inc(kept, 1)

            keep(0)
            for c in range(CHUNKS):
                act.wait_ge(hidden, c + 1)
                act.activation(hid_t[:, c % 2, :].rearrange("p (a n) -> p a n", a=2), up,
                               ACT.Relu if first else ACT.Gelu_apprx_tanh, bias=b1).then_inc(active, 1)
                if c + 1 < CHUNKS:
                    keep(c + 1)
                if not first:
                    act.wait_ge(biased, c + 1)
                    act.activation(t2[:, :], t[:, :], ACT.Gelu_apprx_tanh).then_inc(gelued, 1)
                act.wait_ge(S["var_ready"], c + 1)
                act.activation(S["root"][:, :], S["var"][:, :], ACT.Sqrt).then_inc(rooted, 1)

        if not first:
            @block.sync
            def _(sp):
                for c in range(CHUNKS):
                    sp.wait_ge(normed, c + 1)
                    sp.dma_start(dram["x2"][c * CHUNK * P:(c + 1) * CHUNK * P, :].rearrange("(b p) d -> p b d", p=P),
                                 S["x"][:, c * CW:(c + 1) * CW].rearrange("p (b d) -> p b d", d=D)).then_inc(saved, 16)
                sp.wait_ge(saved, 16 * CHUNKS)


def project(nc, S, dram):
    with ExitStack() as stack:
        m = Memory(nc, stack)
        xs, x_t = m.sb("qkv_xs", [P, CW]), m.sb("qkv_xT", [P, CW])
        kv = m.sb("qkv_kv", [P, CHUNK, 2 * D])
        staged, turned, kept, product, split, saved = (m.sem("qkv_" + n) for n in (
            "staged", "turned", "kept", "product", "split", "saved"))
        ps = S["ps"]
        outs = ps[:, 2 * BANK:(2 + CHUNK) * BANK].rearrange("p (b n) -> p b n", b=CHUNK)
        block = stack.enter_context(nc.Block())

        @block.scalar
        def _(act):
            with act.Fori(0, CHUNKS) as i:
                act.wait_ge(split, i * 3 + 1)
                act.nop(nofuse=True)
                act.activation(xs[:, :], chunk_of(S["x"], i), ACT.Copy).then_inc(staged, 1)
                act.wait_ge(turned, i + 1)
                act.activation(x_t[:, :], ps[:, 0:CW], ACT.Copy).then_inc(kept, 1)

        @block.tensor
        def _(pe):
            with pe.Fori(0, CHUNKS) as i:
                pe.wait_ge(staged, i + 1)
                for b in range(CHUNK):
                    last = pe.transpose(ps[:, b * D:(b + 1) * D], xs[:, b * D:(b + 1) * D], S["ident"][:, :])
                last.then_inc(turned, 1)
                pe.wait_ge(kept, i + 1)
                for b in range(CHUNK):
                    last = pe.matmul(outs[:, b, :], x_t[:, b * D:(b + 1) * D], S["w_qkvs"][:, :], start=True, stop=True)
                last.then_inc(product, 1)

        @block.vector
        def _(dve):
            dve.sem_inc(split, 1)
            dve.sem_inc(saved, 16)
            with dve.Fori(0, CHUNKS) as i:
                dve.wait_ge(product, i + 1)
                for dest, lo, hi in ((chunk_of(S["q"], i).rearrange("p (b d) -> p b d", d=D), 0, D), (kv[:, :, :], D, 3 * D),
                                     (chunk_of(S["skip"], i).rearrange("p (b d) -> p b d", d=D), 3 * D, 4 * D)):
                    if hi - lo > D:
                        dve.wait_ge(saved, (i + 1) * 16)
                    dve.tensor_tensor(dest, outs[:, :, lo:hi],
                                      S["b_row"][:, lo:hi].unsqueeze(1).to_broadcast([P, CHUNK, hi - lo]), ALU.add).then_inc(split, 1)

        @block.sync
        def _(sp):
            with sp.Fori(0, CHUNKS) as i:
                sp.wait_ge(split, i * 3 + 4)
                sp.dma_start(dram["kv"][bass.ds(i * (CHUNK * P), CHUNK * P), :].rearrange("(b p) d -> p b d", p=P),
                             kv[:, :, :]).then_inc(saved, 16)
            sp.wait_ge(saved, 16 * (CHUNKS + 1))


def scores(nc, S, dram):
    STEP = P // EDGE_DIM
    WAYS = 4
    WHOLE = PAIRS_PAD // (WAYS * STEP)
    with ExitStack() as stack:
        m = Memory(nc, stack)
        kv = m.sb("sc_kv", [P, WAYS, STEP, 2 * D])
        kve = m.sb("sc_kve", [P, WAYS, STEP, 2 * D])
        attr = m.sb("sc_attr", [P, WAYS, STEP * EDGE_DIM])
        attr_t = m.sb("sc_attrT", [P, 2, P])
        locb = m.sb("sc_locb", [P, WAYS, STEP * P])
        hot_t = m.sb("sc_hotT", [P, WAYS, STEP * P])
        prod = m.sb("sc_prod", [P, 2, STEP * D])
        cur = m.sb("sc_cur", [P, WAYS * STEP], I32)
        landed, copied, featured, placed, turned, kept, heated, product, added, multiplied, scored, saved = (
            [m.sem(f"sc_{n}{h}") for h in range(WAYS)] for n in ("landed", "copied", "featured", "placed", "turned",
            "kept", "heated", "product", "added", "multiplied", "scored", "saved"))
        cleared = m.sem("sc_cleared")
        ps = S["ps"]
        block = stack.enter_context(nc.Block())

        def qe(q):
            return ps[:, (q % 2) * 2 * BANK:(q % 2) * 2 * BANK + STEP * D]

        def feat(q):
            return ps[:, (q % 2) * 2 * BANK + BANK:(q % 2) * 2 * BANK + BANK + STEP * D]

        def turn(q):
            return ps[:, (4 + q % 2) * BANK:(4 + q % 2) * BANK + P]

        def before_last(eng, sems, q, i):
            if q < 2:
                eng.wait_ge(sems[q + 2], i + 1)
            else:
                eng.wait_ge(sems[q - 2], i + 2)

        @block.gpsimd
        def _(pool):
            def index(i, q):
                pool.tensor_copy(cur[:, q * STEP:(q + 1) * STEP],
                                 S["d_src"][:, bass.ds(i * (WAYS * STEP) + q * STEP, STEP)]).then_inc(copied[q], 1)

            pool.wait_ge(added[0], 1)
            index(0, 0)
            with pool.Fori(0, WHOLE) as i:
                for q in range(WAYS):
                    ahead, n = (i, q + 1) if q + 1 < WAYS else (i + 1, 0)
                    pool.wait_ge(added[n], ahead + 1)
                    pool.nop(nofuse=True)
                    index(ahead, n)
                    pool.wait_ge(copied[q], i + 1)
                    pool.nop(nofuse=True)
                    for j in range(STEP):
                        c = q * STEP + j
                        pool.indirect_dma_start(out=kv[:, q, j, :], out_offset=None, in_=dram["kv"],
                                                in_offset=bass.IndirectOffsetOnAxis(ap=cur[:, c:c + 1], axis=0)).then_inc(landed[q], 16)

        @block.sync
        def _(sp):
            with sp.Fori(0, WHOLE) as i:
                for q in range(WAYS):
                    start = i * (WAYS * STEP) + q * STEP
                    _, rows = nc.values_load_multi_w_load_instructions(
                        S["dst_steps"][0:1, bass.ds(start + 2 * PAIR_COLS, STEP)], engines=[mybir.EngineType.SP], min_val=0,
                        max_val=(TILES - 1) * P, skip_runtime_bounds_check_because="tile numbers capped when they were made")
                    sp.wait_ge(turned[q], i + 1)
                    for j in range(STEP):
                        sp.dma_start(attr[:, q, j * EDGE_DIM:(j + 1) * EDGE_DIM],
                                     dram["attr"][bass.ds(rows[j], P), :]).then_inc(featured[q], 16)
                    sp.wait_ge(heated[q], i + 1)
                    sp.dma_start(locb[:, q, :], dram["loc"][bass.ds(start, STEP), :].rearrange("(a k) e -> a (k e)", a=1)
                                 .to_broadcast([P, STEP * P])).then_inc(placed[q], 16)

        @block.scalar
        def _(act):
            for q in range(WAYS):
                act.sem_inc(saved[q], 16)
            with act.Fori(0, WHOLE) as i:
                for q in range(WAYS):
                    act.wait_ge(turned[q], i + 2)
                    before_last(act, product, q, i)
                    act.activation(attr_t[:, q % 2, :], turn(q), ACT.Copy).then_inc(kept[q], 1)
                    act.wait_ge(added[q], i + 2)
                    act.dma_start(dram["ve"][bass.ds(i * (WAYS * STEP) + q * STEP, STEP), :, :].rearrange("k e d -> e k d"),
                                  kve[:, q, :, D:2 * D]).then_inc(saved[q], 16)
            for q in range(WAYS):
                act.wait_ge(saved[q], 16 * (WHOLE + 1))

        @block.vector
        def _(dve):
            dve.memset(S["alpha"][:, :, :], 0.0).then_inc(cleared, 1)
            dve.wait_ge(cleared, 1)
            for q in range(WAYS):
                for s in (heated, added, scored, kept):
                    dve.sem_inc(s[q], 1)

            def heat(i, q):
                dve.wait_ge(placed[q], (i + 1) * 16)
                dve.wait_ge(product[q], i + 1)
                dve.tensor_scalar(hot_t[:, q, :], locb[:, q, :], S["part"][:, 0:1], None, ALU.is_equal).then_inc(heated[q], 1)

            def score(i, q):
                dve.wait_ge(landed[q], (i + 1) * (16 * STEP))
                dve.wait_ge(product[q], i + 2)
                dve.wait_ge(saved[q], (i + 1) * 16)
                dve.tensor_tensor(kve[:, q].rearrange("p k (a d) -> p k a d", a=2), kv[:, q].rearrange("p k (a d) -> p k a d", a=2),
                                  feat(q).rearrange("p (k d) -> p k d", d=D).unsqueeze(2).to_broadcast([P, STEP, 2, D]),
                                  ALU.add).then_inc(added[q], 1)
                dve.wait_ge(added[q], i + 2)
                dve.tensor_tensor(prod[:, q % 2, :].rearrange("p (k d) -> p k d", d=D), qe(q).rearrange("p (k d) -> p k d", d=D),
                                  kve[:, q, :, 0:D], ALU.mult).then_inc(multiplied[q], 1)
                dve.wait_ge(multiplied[q], i + 1)
                dve.tensor_reduce(S["alpha"][:, :, bass.ds(i * (WAYS * STEP) + q * STEP, STEP)].rearrange("p a k -> p k a"),
                                  prod[:, q % 2, :].rearrange("p (k a c) -> p k a c", a=HEADS, c=HEAD), AX.X, ALU.add).then_inc(scored[q], 1)

            with dve.Fori(0, WHOLE) as i:
                heat(i, 0)
                heat(i, 1)
                for q in range(WAYS):
                    if q + 2 < WAYS:
                        heat(i, q + 2)
                    score(i, q)
            for q in range(WAYS):
                dve.wait_ge(scored[q], WHOLE + 1)

        @block.tensor
        def _(pe):
            for q in range(WAYS):
                pe.sem_inc(turned[q], 1)
                pe.sem_inc(product[q], 1)
            with pe.Fori(0, WHOLE) as i:
                for q in range(WAYS):
                    start = i * (WAYS * STEP) + q * STEP
                    _, cols = nc.values_load_multi_w_load_instructions(
                        S["dst_steps"][0:1, bass.ds(start + PAIR_COLS, STEP)], engines=[mybir.EngineType.PE], min_val=0,
                        max_val=(BLOCKS - 1) * D, skip_runtime_bounds_check_because="block numbers are counts of blocks")
                    pe.wait_ge(featured[q], (i + 1) * (16 * STEP))
                    before_last(pe, kept, q, i)
                    pe.transpose(turn(q), attr[:, q, :], S["ident"][:, :]).then_inc(turned[q], 1)
                    before_last(pe, scored, q, i)
                    pe.wait_ge(heated[q], i + 2)
                    for j in range(STEP):
                        pe.matmul(qe(q)[:, j * D:(j + 1) * D], hot_t[:, q, j * P:(j + 1) * P],
                                  S["q"][:, bass.ds(cols[j], D)], start=True, stop=True)
                    pe.wait_ge(kept[q], i + 2)
                    pe.matmul(feat(q), attr_t[:, q % 2, :], S["w_e"][:, :], start=True, stop=True).then_inc(product[q], 1)


def softmax_maxima(nc, S, dram):
    L = PAIRS_PAD
    HR = HEADS * PAIR_BLOCKS
    with ExitStack() as stack:
        m = Memory(nc, stack)
        turn = m.sb("mx_turn", [P, HR, P])
        node = m.sb("mx_node", [P, L])
        node_b = m.sb("mx_before", [P, L])
        node_a = m.sb("mx_after", [P, L])
        loc = m.sb("mx_loc", [P, L])
        bad = m.sb("mx_bad", [P, L])
        score = m.sb("mx_score", [P, HEADS, L])
        top = m.sb("mx_top", [P, HEADS, L])
        both = m.sb("mx_both", [P, L])
        ends = m.sb("mx_ends", [P, 2 * HEADS])
        anyc = m.sb("mx_any", [P, 1])
        over = m.sb("mx_over", [HEADS, 2, P])
        cross = m.sb("mx_cross", [HEADS, P + 1])
        into = m.sb("mx_into", [P, HEADS])
        front = m.sb("mx_front", [1, 1])
        turned, kept, stored, loaded, order, asked, told, ready, exped, done = (m.sem("mx_" + n) for n in (
            "turned", "kept", "stored", "loaded", "order", "asked", "told", "ready", "exped", "done"))
        fronted = m.sem("mx_fronted")
        ps = S["ps"]
        HALF_T = 14
        block = stack.enter_context(nc.Block())
        flat_alpha = dram["alpha"].rearrange("h b e -> h (b e)")
        flat_loc = dram["loc"].rearrange("b e -> (b e)")

        @block.tensor
        def _(pe):
            for n in range(HR):
                h, c = divmod(n, PAIR_BLOCKS)
                if n >= 4:
                    pe.wait_ge(kept, n - 3)
                pe.transpose(ps[:, (n % 4) * BANK:(n % 4) * BANK + P], S["alpha"][:, h, c * P:(c + 1) * P], S["ident"][:, :]).then_inc(turned, 1)
            for way in range(2):
                pe.wait_ge(asked, 2 * way + 1)
                pe.transpose(ps[0:HEADS, 4 * BANK:4 * BANK + P], ends[:, 0:HEADS], S["ident"][:, :])
                pe.transpose(ps[0:HEADS, 4 * BANK + P:4 * BANK + 2 * P], ends[:, HEADS:2 * HEADS], S["ident"][:, :]).then_inc(told, 1)
                pe.wait_ge(asked, 2 * way + 2)
                src = cross[:, 0:P] if way == 0 else cross[:, 1:P + 1]
                pe.transpose(ps[:, 5 * BANK:5 * BANK + HEADS], src, S["ident"][0:HEADS, 0:HEADS]).then_inc(told, 1)
            for n in range(HR):
                h, c = divmod(n, PAIR_BLOCKS)
                if n == 0:
                    pe.wait_ge(loaded, 16 * (4 + HEADS + HR))
                if n >= 4:
                    pe.wait_ge(done, n - 3)
                pe.transpose(ps[:, (n % 4) * BANK:(n % 4) * BANK + P], turn[:, n, :], S["ident"][:, :]).then_inc(turned, 1)

        @block.scalar
        def _(act):
            for n in range(HR):
                act.wait_ge(turned, n + 1)
                act.activation(turn[:, n, :], ps[:, (n % 4) * BANK:(n % 4) * BANK + P], ACT.Copy,
                               scale=float(HEAD) ** -0.5).then_inc(kept, 1)
            for h in range(HEADS):
                act.wait_ge(ready, h + 1)
                act.activation(score[:, h, :], score[:, h, :], ACT.Exp).then_inc(exped, 1)
            for n in range(HR):
                h, c = divmod(n, PAIR_BLOCKS)
                act.wait_ge(turned, HR + n + 1)
                act.activation(S["alpha"][:, h, c * P:(c + 1) * P], ps[:, (n % 4) * BANK:(n % 4) * BANK + P], ACT.Copy).then_inc(done, 1)
            act.wait_ge(done, HR)

        @block.sync
        def _(sp):
            sp.wait_ge(fronted, 1)
            sp.dma_start(dram["node"][0:1].rearrange("(a n) -> a n", a=1), front[:, :]).then_inc(stored, 16)
            for h in range(HEADS):
                sp.wait_ge(kept, (h + 1) * PAIR_BLOCKS)
                sp.dma_start(dram["alpha"][h].rearrange("(c p) e -> p c e", p=P),
                             turn[:, h * PAIR_BLOCKS:(h + 1) * PAIR_BLOCKS, :]).then_inc(stored, 16)
            sp.wait_ge(stored, 16 * (1 + HEADS))
            for t, a in ((node_b, dram["node"][0:P * L]), (node, dram["node"][1:1 + P * L]),
                         (node_a, dram["node"][2:2 + P * L]), (loc, flat_loc[0:P * L])):
                sp.dma_start(t[:, :], a.rearrange("(p c) -> p c", p=P)).then_inc(loaded, 16)
            for h in range(HEADS):
                sp.dma_start(score[:, h, :], flat_alpha[h, 0:P * L].rearrange("(p c) -> p c", p=P)).then_inc(loaded, 16)
            for h in range(HEADS):
                sp.wait_ge(exped, h + 1)
                sp.dma_start(flat_alpha[h, 0:P * L].rearrange("(p c) -> p c", p=P), score[:, h, :]).then_inc(stored, 16)
            sp.wait_ge(stored, 16 * (1 + 2 * HEADS))
            for h in range(HEADS):
                for c in range(PAIR_BLOCKS):
                    sp.dma_start(turn[:, h * PAIR_BLOCKS + c, :], dram["alpha"][h, c * P:(c + 1) * P, :]).then_inc(loaded, 16)

        @block.vector
        def _(dve):
            link = Chain(dve, order)
            dve.memset(front[:, :], -1.0).then_inc(fronted, 1)
            dve.wait_ge(loaded, 16 * (4 + HEADS))
            link(dve.tensor_scalar(bad[:, :], loc[:, :], 0.0, None, ALU.is_lt))
            link(dve.tensor_scalar(loc[:, :], loc[:, :], float(P), None, ALU.is_ge))
            link(dve.tensor_tensor(bad[:, :], bad[:, :], loc[:, :], ALU.add))
            for h in range(HEADS):
                link(dve.scalar_tensor_tensor(score[:, h, :], bad[:, :], -BIG, score[:, h, :], ALU.mult, ALU.add))
            link(dve.tensor_tensor(node_b[:, :], node_b[:, :], node[:, :], ALU.not_equal))
            link(dve.tensor_tensor(node_a[:, :], node_a[:, :], node[:, :], ALU.not_equal))
            for way, edge in enumerate((node_b, node_a)):
                link(dve.tensor_reduce(anyc[:, :], edge[:, :], AX.X, ALU.max))
                link(dve.tensor_scalar_mul(edge[:, :], edge[:, :], -BIG))
                link(dve.tensor_scalar_mul(ends[:, HEADS:2 * HEADS], anyc[:, :].to_broadcast([P, HEADS]), -BIG))
                src = score if way == 0 else top

                def run(a):
                    return a if way == 0 else a[:, ::-1]
                edge_last = L - 1 if way == 0 else 0
                for h in range(HEADS):
                    link(dve.tensor_tensor_scan(run(both[:, :]), run(edge[:, :]), run(src[:, h, :]), -BIG, ALU.add, ALU.max))
                    link(dve.tensor_copy(ends[:, h:h + 1], both[:, edge_last:edge_last + 1]))
                dve.engine_nop().then_inc(asked, 1)
                dve.wait_ge(told, 2 * way + 1)
                link(dve.tensor_copy(over[:, :, :], ps[0:HEADS, 4 * BANK:4 * BANK + 2 * P].rearrange("p (a n) -> p a n", a=2)))
                if way == 0:
                    link(dve.memset(cross[:, 0:1], -BIG))
                    link(dve.tensor_tensor_scan(cross[:, 1:P + 1], over[:, 1, :], over[:, 0, :], -BIG, ALU.add, ALU.max))
                else:
                    link(dve.memset(cross[:, P:P + 1], -BIG))
                    link(dve.tensor_tensor_scan(cross[:, 0:P][:, ::-1], over[:, 1, ::-1], over[:, 0, ::-1], -BIG, ALU.add, ALU.max))
                dve.engine_nop().then_inc(asked, 1)
                dve.wait_ge(told, 2 * way + 2)
                link(dve.tensor_copy(into[:, :], ps[:, 5 * BANK:5 * BANK + HEADS]))
                for h in range(HEADS):
                    dest = top[:, h, :] if way == 0 else both[:, :]
                    link(dve.tensor_tensor_scan(run(dest), run(edge[:, :]), run(src[:, h, :]), into[:, h:h + 1], ALU.add, ALU.max))
                    if way == 1:
                        link(dve.tensor_tensor(score[:, h, :], score[:, h, :], both[:, :], ALU.subtract))
                        dve.engine_nop().then_inc(ready, 1)


def weigh_values(nc, S, dram):
    with ExitStack() as stack:
        m = Memory(nc, stack)
        ve = m.sb("wv_ve", [P, 2, GROUP, D])
        pv = m.sb("wv_pv", [P, 2, GROUP, AW])
        hot = m.sb("wv_hot", [P, 2, GROUP, P])
        landed, weighed, summed, added, heated, copied, acc_order = ([m.sem(f"wv_{n}{h}") for h in range(2)] for n in (
            "landed", "weighed", "summed", "added", "hot", "copied", "acc"))
        cleared = m.sem("wv_cleared")
        sums = [S["sums"], m.sb("wv_odd", [P, BLOCKS * AW])]
        block = stack.enter_context(nc.Block())

        @block.sync
        def _(sp):
            with sp.Fori(0, ROUNDS) as i:
                for h in range(2):
                    sp.wait_ge(weighed[h], i + 1)
                    sp.dma_start(ve[:, h], dram["ve"][bass.ds(i * (2 * GROUP) + h * GROUP, GROUP), :, :]
                                 .rearrange("k e d -> e k d")).then_inc(landed[h], 16)

        @block.gpsimd
        def _(pool):
            with pool.Fori(0, ROUNDS) as i:
                for h in range(2):
                    pool.wait_ge(summed[h], i + 1)
                    pool.nop(nofuse=True)
                    pool.wait_ge(landed[h], (i + 1) * 16)
                    pool.nop(nofuse=True)
                    pool.tensor_tensor(pv[:, h, :, 0:D].rearrange("p k (a c) -> p k a c", c=HEAD),
                                       ve[:, h].rearrange("p k (a c) -> p k a c", c=HEAD),
                                       S["alpha"][:, :, bass.ds(i * (2 * GROUP) + h * GROUP, GROUP)].rearrange("p a k -> p k a")
                                       .unsqueeze(3).to_broadcast([P, GROUP, HEADS, HEAD]), ALU.mult).then_inc(weighed[h], 1)

        @block.scalar
        def _(act):
            with act.Fori(0, ROUNDS) as i:
                for h in range(2):
                    act.wait_ge(summed[h], i + 1)
                    act.nop(nofuse=True)
                    act.activation(pv[:, h, :, D:AW], S["alpha"][:, :, bass.ds(i * (2 * GROUP) + h * GROUP, GROUP)]
                                   .rearrange("p a k -> p k a"), ACT.Copy).then_inc(copied[h], 1)

        @block.vector
        def _(dve):
            dve.memset(sums[0][:, :], 0.0).then_inc(cleared, 1)
            dve.memset(sums[1][:, :], 0.0).then_inc(cleared, 1)
            dve.wait_ge(cleared, 2)
            for k in range(2):
                dve.sem_inc(acc_order[k], 1)
                dve.sem_inc(added[k], 1)
                dve.sem_inc(weighed[k], 1)

            def heat(i, h):
                dve.tensor_tensor(hot[:, h], S["col"][:, :].unsqueeze(1).to_broadcast([P, GROUP, P]),
                                  S["dst_loc"][:, bass.ds(i * (2 * GROUP) + h * GROUP, GROUP)].unsqueeze(2)
                                  .to_broadcast([P, GROUP, P]), ALU.is_equal).then_inc(heated[h], 1)

            heat(0, 0)
            heat(0, 1)
            with dve.Fori(0, ROUNDS) as i:
                for h in range(2):
                    columns = load_columns(nc, S, mybir.EngineType.DVE, "dst", 0, i * (2 * GROUP) + h * GROUP)
                    dve.wait_ge(summed[h], i + 2)
                    heat(i + 1, h)
                    for j, (part, col) in enumerate(zip(pairs_of(S["ps"], h, AW), columns)):
                        k, n = j % 2, j // 2
                        dve.wait_ge(acc_order[k], i * GROUP + h * (GROUP // 2) + n + 1)
                        dve.tensor_tensor(sums[k][:, bass.ds(col, AW)], sums[k][:, bass.ds(col, AW)], part, ALU.add).then_inc(acc_order[k], 1)
                    for k in range(2):
                        dve.wait_ge(acc_order[k], i * GROUP + (h + 1) * (GROUP // 2) + 1)
                    dve.sem_inc(added[h], 1)
            dve.tensor_tensor(sums[0][:, :], sums[0][:, :], sums[1][:, :], ALU.add).then_inc(cleared, 1)
            dve.wait_ge(cleared, 3)

        @block.tensor
        def _(pe):
            for h in range(2):
                pe.sem_inc(summed[h], 1)
            with pe.Fori(0, ROUNDS) as i:
                for h in range(2):
                    pe.wait_ge(heated[h], i + 1)
                    pe.wait_ge(copied[h], i + 1)
                    pe.wait_ge(added[h], i + 1)
                    pe.wait_ge(weighed[h], i + 2)
                    for j, part in enumerate(pairs_of(S["ps"], h, AW)):
                        last = pe.matmul(part, hot[:, h, j, :], pv[:, h, j, :], start=True, stop=True)
                    last.then_inc(summed[h], 1)


def residual_norm(nc, S, dram, tag, light, out=None):
    with ExitStack() as stack:
        m = Memory(nc, stack)
        t = m.sb(tag + "_t", [P, BLOCKS * D])
        stats = m.sb(tag + "_stats", [P, BLOCKS, 6])
        moments = m.sb(tag + "_moments", [P, BLOCKS, 2])
        var, root, rstd = (m.sb(tag + n, [P, BLOCKS]) for n in ("_var", "_root", "_rstd"))
        varied, rooted, order, normed, saved = (m.sem(f"{tag}_{n}") for n in ("varied", "rooted", "order", "normed", "saved"))
        block = stack.enter_context(nc.Block())

        @block.vector
        def _(dve):
            link = Chain(dve, order)
            tv = t[:, :].rearrange("p (b d) -> p b d", d=D)
            x = S["x"][:, :].rearrange("p (b d) -> p b d", d=D)
            sums = S["sums"][:, :].rearrange("p (b w) -> p b w", w=AW)[:, :, 0:D]
            if light:
                link(dve.scalar_tensor_tensor(tv, sums, 3.0, x, ALU.mult, ALU.add))
                link(dve.scalar_tensor_tensor(tv, tv, 0.25, x, ALU.mult, ALU.add))
            else:
                link(dve.tensor_tensor(tv, sums, x, ALU.add))
            for b in range(BLOCKS):
                last = dve.bn_stats(stats[:, b, :], tv[:, b, :])
            link(last)
            for b in range(BLOCKS):
                last = dve.bn_aggr(moments[:, b, :], stats[:, b, :])
            link(last)
            dve.tensor_scalar_add(var[:, :], moments[:, :, 1], EPS).then_inc(varied, 1)
            dve.wait_ge(rooted, 1)
            link(dve.reciprocal(rstd[:, :], root[:, :]))
            for b in range(BLOCKS):
                dve.tensor_scalar(x[:, b, :], tv[:, b, :], moments[:, b, 0:1], rstd[:, b:b + 1],
                                  ALU.subtract, ALU.mult).then_inc(normed, 1)
            dve.wait_ge(normed, BLOCKS)

        @block.scalar
        def _(act):
            act.wait_ge(varied, 1)
            act.activation(root[:, :], var[:, :], ACT.Sqrt).then_inc(rooted, 1)

        if out is not None:
            @block.sync
            def _(sp):
                whole, cut = (BLOCKS - 1) * P, BLOCKS // 2
                for lo, hi in ((0, cut), (cut, BLOCKS - 1)):
                    sp.wait_ge(normed, hi)
                    sp.dma_start(out[lo * P:hi * P, :].rearrange("(b p) d -> p b d", p=P),
                                 S["x"][:, lo * D:hi * D].rearrange("p (b d) -> p b d", d=D)).then_inc(saved, 16)
                sp.wait_ge(normed, BLOCKS)
                sp.dma_start(out[whole:N, :], S["x"][0:N - whole, (BLOCKS - 1) * D:]).then_inc(saved, 16)
                sp.wait_ge(saved, 48)


def messages(nc, S, dram, weights, biases):
    PIECES = -(-RW // BANK)
    BUFS = PIECES
    with ExitStack() as stack:
        m = Memory(nc, stack)
        w = m.sb("ms_w", [P, RW])
        bias = m.sb("ms_b", [P, RW])
        xs, x_t = m.sb("ms_xs", [P, CW]), m.sb("ms_xT", [P, CW])
        y = m.sb("ms_y", [P, 2, RW])
        loaded, staged, turned, kept, product, biased = (m.sem("ms_" + n) for n in (
            "loaded", "staged", "turned", "kept", "product", "biased"))
        saved = [m.sem(f"ms_saved{k}") for k in range(2)]
        ps = S["ps"]
        last_layer = weights.shape[0] - 1
        block = stack.enter_context(nc.Block())

        @block.sync
        def _(sp):
            sp.dma_start(w[:, :].rearrange("p (r h) -> p r h", h=D), weights[last_layer].rearrange("r e h -> e r h")).then_inc(loaded, 16)
            sp.dma_start(bias[:, :], biases[last_layer].rearrange("(a r) h -> a (r h)", a=1).to_broadcast([P, RW])).then_inc(loaded, 16)
            for k in range(2):
                sp.sem_inc(saved[k], 16)
            with sp.Fori(0, BLOCKS // CHUNK) as i:
                for b in range(CHUNK):
                    sp.wait_ge(biased, i * (CHUNK * PIECES) + (b + 1) * PIECES + BUFS)
                    sp.dma_start(dram["y"][bass.ds(i * (CHUNK * P) + b * P, P), :], y[:, 0, :] if b % 2 == 0 else y[:, 1, :]).then_inc(saved[b % 2], 16)
            sp.wait_ge(saved[0], 16 * (1 + 3 * CHUNKS))
            sp.wait_ge(saved[1], 16 * (1 + 2 * CHUNKS))

        @block.scalar
        def _(act):
            with act.Fori(0, CHUNKS) as i:
                act.wait_ge(product, i * (CHUNK * PIECES) + 1)
                act.nop(nofuse=True)
                act.activation(xs[:, :], chunk_of(S["x"], i), ACT.Copy).then_inc(staged, 1)
                act.wait_ge(turned, i + 1)
                act.activation(x_t[:, :], ps[:, 0:CW], ACT.Copy).then_inc(kept, 1)

        @block.tensor
        def _(pe):
            pe.wait_ge(loaded, 32)
            pe.sem_inc(product, 1)
            with pe.Fori(0, CHUNKS) as i:
                pe.wait_ge(staged, i + 1)
                for b in range(CHUNK):
                    last = pe.transpose(ps[:, b * D:(b + 1) * D], xs[:, b * D:(b + 1) * D], S["ident"][:, :])
                last.then_inc(turned, 1)
                pe.wait_ge(kept, i + 1)
                for b in range(CHUNK):
                    for k in range(PIECES):
                        n = b * PIECES + k
                        cols = min(BANK, RW - k * BANK)
                        bank = 2 + n % BUFS
                        pe.wait_ge(biased, i * (CHUNK * PIECES) + n + 1)
                        pe.matmul(ps[:, bank * BANK:bank * BANK + cols], x_t[:, b * D:(b + 1) * D],
                                  w[:, k * BANK:k * BANK + cols], start=True, stop=True).then_inc(product, 1)

        @block.vector
        def _(dve):
            dve.sem_inc(biased, BUFS)
            dve.wait_ge(loaded, 32)
            with dve.Fori(0, CHUNKS) as i:
                for b in range(CHUNK):
                    before = i * 3 + b // 2 if b % 2 == 0 else i * 2 + b // 2
                    dve.wait_ge(saved[b % 2], (before + 1) * 16)
                    for k in range(PIECES):
                        n = b * PIECES + k
                        cols = min(BANK, RW - k * BANK)
                        bank = 2 + n % BUFS
                        dve.wait_ge(product, i * (CHUNK * PIECES) + n + 2)
                        dve.tensor_tensor(y[:, b % 2, k * BANK:k * BANK + cols], ps[:, bank * BANK:bank * BANK + cols],
                                          bias[:, k * BANK:k * BANK + cols], ALU.add).then_inc(biased, 1)


def gnn_kernel(nc, ins, out):
    def scratch(name, shape, dt=F32):
        return nc.dram_tensor(name, shape, dt, kind="Internal").ap()

    dram = {
        "rec_by_dst": scratch("rec_by_dst", [EDGES, REC]), "msg": scratch("msg", [EDGES, MSG]),
        "attr": scratch("attr", [EDGES, EDGE_DIM]), "attr_given": scratch("attr_given", [EDGES, EDGE_DIM]), "base": scratch("base", [PAIR_COLS]),
        "steps": scratch("steps", [3, PAIR_COLS], I32), "loc": scratch("loc", [PAIR_COLS, P]),
        "node": scratch("node", [PAIR_COLS * P + P]), "kv": scratch("kv", [ROWS, 2 * D]),
        "ve": scratch("ve", [PAIRS_PAD, P, D]), "alpha": scratch("alpha", [HEADS, PAIR_COLS, P]),
        "x2": scratch("x2", [ROWS, D]), "y": scratch("y", [ROWS, RW]),
    }
    Memory.spent = []
    with ExitStack() as stack:
        m = Memory(nc, stack)
        S = {
            "ident": m.sb("ident", [P, P]), "strict": m.sb("strict", [P, P]), "ones": m.sb("ones", [P, P]),
            "col": m.sb("col", [P, P]), "part": m.sb("part", [P, 1]), "flag": m.sb("flag_i", [1, 1], I32),
            "x": m.sb("x_rows", [P, BLOCKS * D]), "sums": m.sb("sums", [P, BLOCKS * AW]),
            "src_loc": m.sb("src_loc", [P, PAIR_COLS]), "s_dst": m.sb("s_dst", [P, PAIR_COLS], I32),
            "s_w": m.sb("s_w", [P, PAIR_COLS]), "s_msg": m.sb("s_msg", [P, PAIR_COLS], I32),
            "dst_loc": m.sb("dst_loc", [P, PAIR_COLS]), "d_src": m.sb("d_src", [P, PAIR_COLS], I32),
            "d_msg": m.sb("d_msg", [P, PAIR_COLS], I32),
            "src_steps": m.sb("src_steps", [1, 3 * PAIR_COLS], I32), "dst_steps": m.sb("dst_steps", [1, 3 * PAIR_COLS], I32),
            "w_l0": m.sb("w_l0", [P, 2 * D]), "w_qkvs": m.sb("w_qkvs", [P, 4 * D]), "w_l1": m.sb("w_l1", [P, 2, D]),
            "w_e": m.sb("w_e", [P, 4 * D]), "b_col": m.sb("b_col", [P, 2]), "b_row": m.sb("b_row", [P, 6 * D]),
            "ps": stack.enter_context(nc.psum_tensor("ps", [P, 8 * BANK], F32)),
        }
        with ExitStack() as first:
            f = Memory(nc, first)
            S["d_rec"] = f.sb("d_rec", [P, PAIR_COLS, 4])
            S["d_place"] = f.sb("d_place", [P, PAIR_COLS], I32)
            S["s_base"] = f.sb("s_base", [P, PAIR_COLS])
            S["attr_moved"], S["w_in_place"] = f.sem("attr_moved"), f.sem("w_in_place")
            with ExitStack() as edges:
                e = Memory(nc, edges)
                S["rec"] = e.sb("rec", [P, TILES * REC])
                S["pos"] = e.sb("pos", [P, TILES], I32)
                S["zero"] = e.sb("zero", [P, EDGE_DIM])
                load_and_record(nc, S, dram, ins["x"], ins["src"], ins["dst"], ins["edge_type_9"], ins["edge_weight"], ins["edge_attr_32"])
                load_weights(nc, S, dram, ins)
                unsorted = nc.values_load(S["flag"][0:1, 0:1], min_val=0, max_val=EDGES)
                with nc.If(unsorted > 0):
                    for eng in (nc.gpsimd, nc.scalar, nc.tensor, nc.vector, nc.sync):
                        eng.nop(nofuse=True)
                    sort_by_key(nc, S, "bydst", 1, ROWS, 0)
                    scatter_records(nc, S, "bydst", dram["rec_by_dst"], dram["attr_given"], dram["attr"])
                    store_records(nc, S, dram, "back", reload=True)
                sort_by_key(nc, S, "bysrc", 0, BLOCKS, 7)
                store_records(nc, S, dram, "out")
                staircase(nc, S, dram, "dst", 1, dram["rec_by_dst"],
                          [(S["d_place"][:, :], 4, "place"), (S["d_src"][:, :], 0, "copy"), (S["d_msg"][:, :], 0, "message")]
                          + [(S["d_rec"][:, :, k], field, what) for k, (field, what) in enumerate(((0, "copy"), (1, "copy"), (1, "back"), (3, "copy")))])
                staircase(nc, S, dram, "src", 0)
            send_rows(nc, S, dram)
            first_sum(nc, S, dram)
        mlp_layer(nc, S, dram, "m0", True)
        Memory.clear(nc)
        with ExitStack() as layer:
            a = Memory(nc, layer)
            S["skip"] = a.sb("skip", [P, BLOCKS * D])
            S["alpha"] = a.sb("alpha_cols", [P, HEADS, PAIR_COLS])
            with ExitStack() as early:
                S["q"] = Memory(nc, early).sb("q", [P, BLOCKS * D])
                project(nc, S, dram)
                scores(nc, S, dram)
            softmax_maxima(nc, S, dram)
            weigh_values(nc, S, dram)
            mlp_layer(nc, S, dram, "m1", False)
        Memory.clear(nc)
        gather_sum(nc, S, "g2", "src", dram["x2"], S["s_dst"], weight=S["s_w"])
        residual_norm(nc, S, dram, "n2", True)
        messages(nc, S, dram, ins["L3_gnn_weights"], ins["L3_gnn_biases"])
        table = dram["y"].rearrange("n (r d) -> (n r) d", d=D)
        gather_sum(nc, S, "g3", "dst", table, S["d_msg"])
        gather_sum(nc, S, "g4", "src", table, S["s_msg"], fresh=False)
        residual_norm(nc, S, dram, "n3", False, out=out)


_INS = ["x", "src", "dst", "edge_attr_32", "edge_type_9", "edge_weight", "L0_gnn_W1", "L0_gnn_b1", "L0_gnn_W2", "L0_gnn_b2",
        "L1_gnn_Wq", "L1_gnn_bq", "L1_gnn_Wk", "L1_gnn_bk", "L1_gnn_Wv", "L1_gnn_bv", "L1_gnn_We", "L1_gnn_Wskip",
        "L1_gnn_bskip", "L1_gnn_W1", "L1_gnn_b1", "L1_gnn_W2", "L1_gnn_b2", "L3_gnn_weights", "L3_gnn_biases"]


def kernel(**inputs):
    import numpy as _np
    import concourse.bacc as _bacc
    from concourse import mybir as _mybir
    from concourse.bass_utils import run_bass_kernel_spmd as _run

    nc = _bacc.Bacc("TRN2", target_bir_lowering=False, num_devices=1)
    arrays, aps = {}, {}
    for name in _INS:
        a = _np.ascontiguousarray(inputs[name])
        arrays[f"in_{name}_dram"] = a
        aps[name] = nc.dram_tensor(f"in_{name}_dram", a.shape, _mybir.dt.from_np(a.dtype), kind="ExternalInput").ap()
    out = nc.dram_tensor("out_0_dram", (N, D), F32, kind="ExternalOutput").ap()
    gnn_kernel(nc, aps, out)
    r = _run(nc, [arrays], core_ids=[0])
    return r.results[0]["out_0_dram"]
```
